# Optimizing a Trainium2 kernel written in Bass

```python
import numpy as np
import jax
import jax.numpy as jnp

def _softmax(x, axis=-1):
    return jax.nn.softmax(x, axis=axis)

def _gelu(x):
    return jax.nn.gelu(x, approximate=True)

def _silu(x):
    return jax.nn.silu(x)

def _sigmoid(x):
    return jax.nn.sigmoid(x)

def _layernorm(x, axis=-1, eps=1e-05):
    m = jnp.mean(x, axis=axis, keepdims=True)
    v = jnp.var(x, axis=axis, keepdims=True)
    return (x - m) / jnp.sqrt(v + eps)

def _scatter_add(tgt, idx, src, axis=0):
    return tgt.at[idx].add(src)

def _segment_sum(src, seg, n):
    return jax.ops.segment_sum(src, seg, n)
kernel_name = 'mk_decoder_postln_d1_seqx_r8_03337e'

def setup_inputs(seed: int=0):
    np.random.seed(seed)
    _w = jnp.asarray

    def _rec_inputs():
        import jax
        import jax.numpy as jnp
        _rk = jax.random.key(seed)
        x = 7.22e-05 + 1 * jax.random.normal(jax.random.fold_in(_rk, 1), (8, 128, 512), jnp.float32)
        _lenS = 128 - jax.random.randint(jax.random.fold_in(_rk, 7), (8,), 0, max(1, 128 // 4) + 1, jnp.int32)
        _lenS2 = 128 - jax.random.randint(jax.random.fold_in(_rk, 8), (8,), 0, max(1, 128 // 4) + 1, jnp.int32)
        _ctx_4096P = jax.random.normal(jax.random.fold_in(_rk, 11), (8, 16, 512), jnp.float32)
        _ctx_4096c = jax.random.dirichlet(jax.random.fold_in(_rk, 511), 0.3 * jnp.ones((16,), jnp.float32), (8, 128))
        _ctx_4096t = jnp.einsum('bsk,bkd->bsd', _ctx_4096c, _ctx_4096P)
        _ctx_4096t = _ctx_4096t * jax.lax.rsqrt(jnp.mean(jnp.square(_ctx_4096t)) + 1e-12) * 0.953939
        ctx_4096 = 4.13588e-05 + 0.999923 * (_ctx_4096t + 0.3 * jax.random.normal(jax.random.fold_in(_rk, 611), (8, 128, 512), jnp.float32))
        _validS = jnp.arange(128)[None, :] < _lenS[:, None]
        _validS2 = jnp.arange(128)[None, :] < _lenS2[:, None]
        _causal = jnp.tril(jnp.ones((128, 128), dtype=bool))
        mask_BxSxS2_bk0 = jnp.logical_not(jnp.broadcast_to(_validS2[:, None, :], (8, 128, 128)))
        return (x, ctx_4096, mask_BxSxS2_bk0)
    x, ctx_4096, mask_BxSxS2_bk0 = _rec_inputs()

    def _L0_attn_setup():
        import math
        import jax, jax.numpy as jnp
        import numpy as np
        B, T, E = (2, 256, 512)
        H, HKV = (32, 8)
        DH = E // H
        G = H // HKV
        ROPE_THETA = 500000.0
        ROPE_FACTOR = 32.0
        HI_FREQ_FACTOR = 4.0
        LO_FREQ_FACTOR = 1.0
        ORIG_CTX = 1024

        def _rope_cos_sin(t_len):
            inv_freq = 1.0 / ROPE_THETA ** (jnp.arange(0, DH, 2, dtype=jnp.float32) / DH)
            wavelen = 2.0 * math.pi / inv_freq
            cut_lo = ORIG_CTX / HI_FREQ_FACTOR
            cut_hi = ORIG_CTX / LO_FREQ_FACTOR
            inv_freq = jnp.where(wavelen > cut_hi, inv_freq / ROPE_FACTOR, inv_freq)
            smooth = (ORIG_CTX / wavelen - LO_FREQ_FACTOR) / (HI_FREQ_FACTOR - LO_FREQ_FACTOR)
            smoothed = (1.0 - smooth) * inv_freq / ROPE_FACTOR + smooth * inv_freq
            is_medium = ~(wavelen < cut_hi) & ~(wavelen > cut_lo)
            inv_freq = jnp.where(is_medium, smoothed, inv_freq)
            pos = jnp.arange(t_len, dtype=jnp.float32)
            freqs = pos[:, None] * inv_freq[None, :]
            emb = jnp.concatenate([freqs, freqs], axis=-1)
            return (jnp.cos(emb), jnp.sin(emb))

        def _rotate_half(x):
            x1, x2 = jnp.split(x, 2, axis=-1)
            return jnp.concatenate([-x2, x1], axis=-1)
        key = jax.random.key(seed)
        kx, kq, kk, kv, ko = jax.random.split(key, 5)
        w = lambda k, shape: jax.random.normal(k, shape, jnp.float32) * 0.02
        return {'x': jax.random.normal(kx, (B, T, E), jnp.float32), 'Wq': w(kq, (E, E)), 'Wk': w(kk, (HKV * DH, E)), 'Wv': w(kv, (HKV * DH, E)), 'Wo': w(ko, (E, E))}
    _L0_attn_all = _L0_attn_setup()
    _L0_attn_in = {k: v for k, v in _L0_attn_all.items() if k in ('Wq', 'Wk', 'Wv', 'Wo')}
    del _L0_attn_all

    def _L0_xattn_setup():
        import jax, jax.numpy as jnp
        import numpy as np
        B, LQ, LK, D, H, DH = (2, 128, 128, 512, 32, 128)
        EPS = 1e-05

        def _rmsnorm(x, weight):
            var = jnp.mean(jnp.square(x), axis=-1, keepdims=True)
            return x * jax.lax.rsqrt(var + EPS) * weight
        key = jax.random.key(seed)
        ks = jax.random.split(key, 8)
        scale = 0.02
        return {'hidden_states': jax.random.normal(ks[0], (B, LQ, D), jnp.float32), 'key_value_states': jax.random.normal(ks[1], (B, LK, D), jnp.float32), 'attention_mask': jax.random.randint(ks[2], (B, LQ, LK), 0, 2) > 0, 'position_bias': jax.random.normal(ks[3], (H, LQ, LK), jnp.float32), 'ln_weight': jnp.ones((D,), jnp.float32), 'w_q': jax.random.normal(ks[4], (H * DH, D), jnp.float32) * scale, 'w_k': jax.random.normal(ks[5], (H * DH, D), jnp.float32) * scale, 'w_v': jax.random.normal(ks[6], (H * DH, D), jnp.float32) * scale, 'w_out': jax.random.normal(ks[7], (D, H * DH), jnp.float32) * scale}
    _L0_xattn_all = _L0_xattn_setup()
    _L0_xattn_in = {k: v for k, v in _L0_xattn_all.items() if k in ('position_bias', 'ln_weight', 'w_q', 'w_k', 'w_v', 'w_out')}
    del _L0_xattn_all

    def _L0_ffn_setup():
        import jax, jax.numpy as jnp
        import numpy as np
        SCALING = 16.0 / 8.0
        GAMMA = 1.0
        EPS = 1e-12
        key = jax.random.key(seed)
        ks = jax.random.split(key, 8)
        B, T, H, O = (4, 256, 512, 512)
        E_tot, E_act, r = (16, 4, 8)
        return {'x': jax.random.normal(ks[0], (B, T, H), jnp.float32), 'W_base': jax.random.normal(ks[1], (O, H), jnp.float32) * 0.02, 'b_base': jax.random.normal(ks[2], (O,), jnp.float32) * 0.02, 'lora_A': jax.random.normal(ks[3], (E_tot, r, H), jnp.float32) * 0.02, 'lora_B': jax.random.normal(ks[4], (E_tot, O, r), jnp.float32) * 0.02, 'router_W': jax.random.normal(ks[5], (E_tot, H), jnp.float32) * 0.02, 'router_b': jax.random.normal(ks[6], (E_tot,), jnp.float32) * 0.02, 'domain_prior': jax.random.uniform(ks[7], (E_tot,), jnp.float32), 'active': jnp.arange(E_act, dtype=jnp.int32)}
    _L0_ffn_all = _L0_ffn_setup()
    _L0_ffn_in = {k: v for k, v in _L0_ffn_all.items() if k in ('W_base', 'b_base', 'lora_A', 'lora_B', 'router_W', 'router_b', 'domain_prior', 'active')}
    del _L0_ffn_all
    return {'x': x, 'ctx_4096': ctx_4096, 'mask_BxSxS2_bk0': mask_BxSxS2_bk0, 'L0_attn_Wq': _L0_attn_in['Wq'], 'L0_attn_Wk': _L0_attn_in['Wk'], 'L0_attn_Wv': _L0_attn_in['Wv'], 'L0_attn_Wo': _L0_attn_in['Wo'], 'L0_xattn_position_bias': _L0_xattn_in['position_bias'], 'L0_xattn_ln_weight': _L0_xattn_in['ln_weight'], 'L0_xattn_w_q': _L0_xattn_in['w_q'], 'L0_xattn_w_k': _L0_xattn_in['w_k'], 'L0_xattn_w_v': _L0_xattn_in['w_v'], 'L0_xattn_w_out': _L0_xattn_in['w_out'], 'L0_ffn_W_base': _L0_ffn_in['W_base'], 'L0_ffn_b_base': _L0_ffn_in['b_base'], 'L0_ffn_lora_A': _L0_ffn_in['lora_A'], 'L0_ffn_lora_B': _L0_ffn_in['lora_B'], 'L0_ffn_router_W': _L0_ffn_in['router_W'], 'L0_ffn_router_b': _L0_ffn_in['router_b'], 'L0_ffn_domain_prior': _L0_ffn_in['domain_prior'], 'L0_ffn_active': _L0_ffn_in['active']}

def reference(x, ctx_4096, mask_BxSxS2_bk0, L0_attn_Wq, L0_attn_Wk, L0_attn_Wv, L0_attn_Wo, L0_xattn_position_bias, L0_xattn_ln_weight, L0_xattn_w_q, L0_xattn_w_k, L0_xattn_w_v, L0_xattn_w_out, L0_ffn_W_base, L0_ffn_b_base, L0_ffn_lora_A, L0_ffn_lora_B, L0_ffn_router_W, L0_ffn_router_b, L0_ffn_domain_prior, L0_ffn_active):
    import jax
    import jax.numpy as jnp

    def _L0_attn_ref(x, Wq, Wk, Wv, Wo):
        import math
        import jax, jax.numpy as jnp
        import numpy as np
        B, T, E = (2, 256, 512)
        H, HKV = (32, 8)
        DH = E // H
        G = H // HKV
        ROPE_THETA = 500000.0
        ROPE_FACTOR = 32.0
        HI_FREQ_FACTOR = 4.0
        LO_FREQ_FACTOR = 1.0
        ORIG_CTX = 1024

        def _rope_cos_sin(t_len):
            inv_freq = 1.0 / ROPE_THETA ** (jnp.arange(0, DH, 2, dtype=jnp.float32) / DH)
            wavelen = 2.0 * math.pi / inv_freq
            cut_lo = ORIG_CTX / HI_FREQ_FACTOR
            cut_hi = ORIG_CTX / LO_FREQ_FACTOR
            inv_freq = jnp.where(wavelen > cut_hi, inv_freq / ROPE_FACTOR, inv_freq)
            smooth = (ORIG_CTX / wavelen - LO_FREQ_FACTOR) / (HI_FREQ_FACTOR - LO_FREQ_FACTOR)
            smoothed = (1.0 - smooth) * inv_freq / ROPE_FACTOR + smooth * inv_freq
            is_medium = ~(wavelen < cut_hi) & ~(wavelen > cut_lo)
            inv_freq = jnp.where(is_medium, smoothed, inv_freq)
            pos = jnp.arange(t_len, dtype=jnp.float32)
            freqs = pos[:, None] * inv_freq[None, :]
            emb = jnp.concatenate([freqs, freqs], axis=-1)
            return (jnp.cos(emb), jnp.sin(emb))

        def _rotate_half(x):
            x1, x2 = jnp.split(x, 2, axis=-1)
            return jnp.concatenate([-x2, x1], axis=-1)
        b, t, _ = x.shape
        q = (x @ Wq.T).reshape(b, t, H, DH).transpose(0, 2, 1, 3)
        k = (x @ Wk.T).reshape(b, t, HKV, DH).transpose(0, 2, 1, 3)
        v = (x @ Wv.T).reshape(b, t, HKV, DH).transpose(0, 2, 1, 3)
        cos, sin = _rope_cos_sin(t)
        cos = cos.astype(x.dtype)[None, None]
        sin = sin.astype(x.dtype)[None, None]
        q = q * cos + _rotate_half(q) * sin
        k = k * cos + _rotate_half(k) * sin
        qg = q.reshape(b, HKV, G, t, DH)
        scores = jnp.einsum('bhgtd,bhkd->bhgtk', qg.astype(jnp.float32), k.astype(jnp.float32)) / math.sqrt(DH)
        causal = jnp.tril(jnp.ones((t, t), dtype=bool))
        scores = jnp.where(causal[None, None, None], scores, jnp.finfo(jnp.float32).min)
        attn = jax.nn.softmax(scores, axis=-1).astype(x.dtype)
        ctx = jnp.einsum('bhgtk,bhkd->bhgtd', attn, v)
        out = ctx.reshape(b, H, t, DH).transpose(0, 2, 1, 3).reshape(b, t, E)
        return out @ Wo.T

    def _L0_xattn_ref(hidden_states, key_value_states, attention_mask, position_bias, ln_weight, w_q, w_k, w_v, w_out):
        import jax, jax.numpy as jnp
        import numpy as np
        B, LQ, LK, D, H, DH = (2, 128, 128, 512, 32, 128)
        EPS = 1e-05

        def _rmsnorm(x, weight):
            var = jnp.mean(jnp.square(x), axis=-1, keepdims=True)
            return x * jax.lax.rsqrt(var + EPS) * weight
        x = _rmsnorm(hidden_states, ln_weight)
        b, lq, _ = x.shape
        lk = key_value_states.shape[1]
        h_q = (x @ w_q.T).reshape(b, lq, H, DH)
        h_k = (key_value_states @ w_k.T).reshape(b, lk, H, DH)
        h_v = (key_value_states @ w_v.T).reshape(b, lk, H, DH)
        score = jnp.einsum('bqhd,bkhd->bhqk', h_q, h_k)
        score = score + position_bias[None]
        m = attention_mask[:, None]
        score = jnp.where(m, score, -jnp.inf)
        score = jax.nn.softmax(score, axis=-1)
        score = jnp.where(m, score, 0.0)
        attn = jnp.einsum('bhqk,bkhd->bqhd', score, h_v).reshape(b, lq, H * DH)
        out = attn @ w_out.T
        return hidden_states + out

    def _L0_ffn_ref(x, W_base, b_base, lora_A, lora_B, router_W, router_b, domain_prior, active):
        import jax, jax.numpy as jnp
        import numpy as np
        SCALING = 16.0 / 8.0
        GAMMA = 1.0
        EPS = 1e-12
        y = jnp.einsum('bth,oh->bto', x, W_base) + b_base
        A = lora_A[active]
        Bm = lora_B[active]
        z = jnp.einsum('bth,erh->bter', x, A)
        contribs = jnp.einsum('bter,eor->bteo', z, Bm) * SCALING
        logits = jnp.einsum('bth,eh->bte', x, router_W) + router_b
        logits = logits[..., active]
        prior = domain_prior[active]
        alpha = jax.nn.softmax(jnp.log(prior + EPS) + logits / GAMMA, axis=-1)
        return y + jnp.einsum('bteo,bte->bto', contribs, alpha)
    x = _layernorm(x + _L0_attn_ref(x, L0_attn_Wq, L0_attn_Wk, L0_attn_Wv, L0_attn_Wo), axis=-1)
    x = _layernorm(x + _L0_xattn_ref(x, ctx_4096, mask_BxSxS2_bk0, L0_xattn_position_bias, L0_xattn_ln_weight, L0_xattn_w_q, L0_xattn_w_k, L0_xattn_w_v, L0_xattn_w_out), axis=-1)
    x = _layernorm(x + _L0_ffn_ref(x, L0_ffn_W_base, L0_ffn_b_base, L0_ffn_lora_A, L0_ffn_lora_B, L0_ffn_router_W, L0_ffn_router_b, L0_ffn_domain_prior, L0_ffn_active), axis=-1)
    return x

_drawn_inputs = setup_inputs


def setup_inputs(seed=0):
    import zlib

    import numpy as np

    out = dict(_drawn_inputs(seed))
    spreads = {'L0_xattn_ln_weight': (1.0, 0.2)}
    factors = {'L0_attn_Wq': 7.158,
     'L0_attn_Wk': 6.356,
     'L0_ffn_b_base': 3.237,
     'L0_ffn_router_W': 6.912,
     'L0_ffn_router_b': 200.0,
     'L0_ffn_domain_prior': 200.0}
    for name, (base, spread) in spreads.items():
        noise = np.random.default_rng([zlib.crc32(name.encode()), seed]).standard_normal(out[name].shape)
        drawn = base * np.exp(spread * noise) if base else spread * noise
        out[name] = jnp.asarray(drawn.astype(out[name].dtype))
    for name, factor in factors.items():
        out[name] = (out[name] * factor).astype(out[name].dtype)
    return out
```

```python
from contextlib import ExitStack

import numpy as np
import concourse.bass as bass
from concourse import mybir

ALU = mybir.AluOpType
ACT = mybir.ActivationFunctionType
AX_X = mybir.AxisListType.X
F32 = mybir.dt.float32
F32R = mybir.dt.float32r
I32 = mybir.dt.int32
U8 = mybir.dt.uint8

P = 128
B, T, D = 8, 128, 512
KC = D // P
H1, G1, DH1 = 32, 8, 16
R1 = H1 // G1
KV1 = G1 * DH1
STK = 4 * DH1
H2, DH2 = 32, 128
HG = 2
NG = H2 // HG
HALF = B // 2
TILES = 2 * HG
E, RK, EA = 16, 8, 4
LN_EPS = 1e-5
PRIOR_EPS = 1e-12
SCALING = 2.0
MASKED = -1.0e30
FLOOR = -1.0e29
PARTS = ((0, 0), (0, 1), (1, 0))


def gate(nc, spare):
    nc.vector.memset(spare, 0.0)


class Chain:

    def __init__(self, eng, sem, start):
        self.eng, self.sem, self.start, self.n = eng, sem, start, 0

    def link(self, ins):
        self.n += 1
        ins.then_inc(self.sem, 1)
        self.eng.wait_ge(self.sem, self.start + self.n)


def build(nc, a):
    out_d = a["out"].rearrange("b t d -> (b t) d")
    with ExitStack() as whole:
        def sb(ctx, name, shape, dt=F32):
            return ctx.enter_context(nc.sbuf_tensor(name, shape, dt))

        def sem(name):
            return whole.enter_context(nc.semaphore(name))

        banks = [whole.enter_context(nc.psum_tensor(f"bank{i}", [P, 512], F32)) for i in range(8)]

        xnT = [sb(whole, f"xnT_{s}", [P, KC, B * T], F32R) for s in ("hi", "lo")]
        acc = sb(whole, "acc", [P, B, D])
        ident = sb(whole, "ident", [P, P])
        spare = sb(whole, "spare", [P, 1])

        self_attention(nc, a, whole, sb, sem, banks, xnT, acc, ident, spare)
        cross_attention(nc, a, whole, sb, sem, banks, xnT, acc, ident, spare)
        experts(nc, a, whole, sb, sem, banks, acc, ident, spare, out_d)


def f32(ap):
    return ap.bitcast(F32)


def self_attention(nc, a, whole, sb, sem, banks, xnT, acc, ident, spare):
    with ExitStack() as ctx:
        w_raw = sb(ctx, "w1_raw", [P, KC, D + 2 * KV1])
        wo_raw = sb(ctx, "wo1_raw", [P, KC, D])
        w = [sb(ctx, f"w1_{s}", [P, KC, D + 2 * KV1], F32R) for s in ("hi", "lo")]
        wo = [sb(ctx, f"wo1_{s}", [P, KC, D], F32R) for s in ("hi", "lo")]
        xT_raw = sb(ctx, "xT_raw", [P, KC, T])
        x_tok = sb(ctx, "x_tok", [P, D])
        xT = [sb(ctx, f"xT_{s}", [P, KC, T], F32R) for s in ("hi", "lo")]
        rope = sb(ctx, "rope", [P, 4, DH1])
        causal = sb(ctx, "causal", [P, T])
        lnw = sb(ctx, "lnw", [P, D])
        rot_a = sb(ctx, "rot_a", [P, D + KV1])
        rot_b = sb(ctx, "rot_b", [P, D + KV1])
        rot = sb(ctx, "rot", [P, D + KV1])
        q3 = sb(ctx, "q3", [P, H1, STK])
        k3 = sb(ctx, "k3", [P, G1, 2, STK])
        q3T = sb(ctx, "q3T", [P, H1 // 2, T], F32R)
        k3T = sb(ctx, "k3T", [P, G1, 2 * T], F32R)
        v1 = sb(ctx, "v1", [P, G1, DH1 + 1])
        sm = sb(ctx, "sm1", [P, 2, R1, T])
        pr = sb(ctx, "pr1", [P, 2, R1, T])
        prT = sb(ctx, "prT1", [P, 2, R1, T])
        mx = sb(ctx, "mx1", [P, 2, R1])
        nmx = sb(ctx, "nmx1", [P, 2, R1])
        rs = sb(ctx, "rs1", [P, H1])
        on = sb(ctx, "on", [P, H1, DH1])
        onT = [sb(ctx, f"onT_{s}", [P, KC, T], F32R) for s in ("hi", "lo")]
        y = sb(ctx, "y1", [P, D])
        x1 = sb(ctx, "x1", [P, D])
        xn = sb(ctx, "xn", [P, D])
        sq = sb(ctx, "sq1", [P, D])
        st = sb(ctx, "st1", [P, 6])
        mv = sb(ctx, "mv1", [P, 2])
        cols = sb(ctx, "cols1", [P, 8])

        Q, KV, TA, TB, SA, SB_, PT, O0 = banks
        tb = [TA, TB]
        s_bank = [SA, SB_]
        o_bank = [O0, KV]

        s_const = sem("a_const_in")
        s_w = sem("a_weights_in")
        s_x = sem("a_x_in")
        s_fill = sem("a_filled")
        s_whi, s_wlo = sem("a_w_hi"), sem("a_w_lo")
        s_xhi, s_xlo = sem("a_x_hi"), sem("a_x_lo")
        s_qkv = sem("a_qkv")
        s_rot = sem("a_rotated")
        s_hi3, s_lo3, s_v1 = sem("a_stack_hi"), sem("a_stack_lo"), sem("a_v1")
        s_t3 = sem("a_stacks_transposed")
        s_q3T, s_k3T = sem("a_q3T"), sem("a_k3T")
        s_s, s_nm, s_p = sem("a_scores"), sem("a_negmax"), sem("a_probs")
        s_pt, s_ptc, s_pv = sem("a_probs_transposed"), sem("a_prT"), sem("a_pv")
        s_on, s_onT, s_onhi, s_onlo = sem("a_on"), sem("a_on_transposed"), sem("a_onT_hi"), sem("a_onT_lo")
        s_y = sem("a_y")
        s_ve, s_rv, s_x1, s_ms, s_ve2, s_rv2 = (sem("a_" + n) for n in
                                                ("var", "rstd_guess", "x1", "meansq", "ms_eps", "rms_guess"))
        s_xn, s_xnT, s_xnhi, s_xnlo = sem("a_xn"), sem("a_xn_transposed"), sem("a_xnT_hi"), sem("a_xnT_lo")
        c_act, c_dve = sem("a_act_chain"), sem("a_dve_chain")
        ACT_CHAIN, DVE_CHAIN = 2, 23

        block = ctx.enter_context(nc.Block())

        @block.sync
        def _(sp):
            sp.dma_start(w_raw[:], a["wqkv1"]).then_inc(s_w, 16)
            sp.dma_start(ident[:], a["ident"]).then_inc(s_const, 16)
            sp.dma_start(rope[:], a["rope"]).then_inc(s_const, 16)
            sp.dma_start(causal[:], a["causal"]).then_inc(s_const, 16)
            sp.dma_start(wo_raw[:], a["wo1"]).then_inc(s_w, 16)
            sp.dma_start(lnw[:], a["lnw"].partition_broadcast(P)).then_inc(s_const, 16)
            with sp.Fori(0, B) as b:
                sp.wait_ge(s_xlo, b)
                sp.dma_start(xT_raw[:], a["xT"][bass.ds(b, 1)].rearrange("b p c t -> p (b c) t")).then_inc(s_x, 16)
                sp.wait_ge(s_rv, b)
                sp.dma_start(x_tok[:], a["x"][bass.ds(b, 1)].rearrange("b t d -> t (b d)")).then_inc(s_x, 16)

        @block.gpsimd
        def _(pool):
            nc.gpsimd.memset(q3[:], 0.0)
            nc.gpsimd.memset(k3[:], 0.0)
            nc.gpsimd.memset(v1[:], 1.0)
            nc.gpsimd.memset(f32(k3T[:]), 0.0).then_inc(s_fill, 1)

        @block.scalar
        def _(act):
            act.wait_ge(s_w, 32)
            nc.scalar.copy(w[0][:], w_raw[:])
            nc.scalar.copy(wo[0][:], wo_raw[:]).then_inc(s_whi, 1)
            act.wait_ge(s_fill, 1)
            with act.Fori(0, B) as b:
                link = Chain(act, c_act, b * ACT_CHAIN)
                act.wait_ge(s_x, 32 * b + 32)
                act.wait_ge(s_qkv, b)
                nc.scalar.copy(xT[0][:], xT_raw[:]).then_inc(s_xhi, 1)
                act.wait_ge(s_rot, b + 1)
                nc.scalar.copy(q3[:, :, 0:2 * DH1].bitcast(F32R).rearrange("p h (two d) -> p h two d", two=2),
                               rot[:, 0:D].rearrange("p (h one d) -> p h one d", one=1, d=DH1)
                               .broadcast_to([P, H1, 2, DH1]))
                nc.scalar.copy(k3[:, :, 0, 0:DH1].bitcast(F32R),
                               rot[:, D:D + KV1].rearrange("p (g d) -> p g d", d=DH1)).then_inc(s_hi3, 1)
                for m in range(4):
                    act.wait_ge(s_t3, 6 * b + m + 1)
                    nc.scalar.copy(q3T[:, 4 * m:4 * m + 4, :],
                                   tb[m % 2][:].rearrange("p (h t) -> p h t", h=4)).then_inc(s_q3T, 1)
                for j in range(G1):
                    n = b * G1 + j
                    act.wait_ge(s_nm, n + 1)
                    if j >= 2:
                        act.wait_ge(s_pt, n - 1)
                    for r in range(R1):
                        e = nc.scalar.activation(pr[:, j % 2, r], sm[:, j % 2, r], ACT.Exp,
                                                 bias=nmx[:, j % 2, r:r + 1])
                    e.then_inc(s_p, 1)
                act.wait_ge(s_onT, b + 1)
                nc.scalar.copy(onT[0][:], TA[:].rearrange("p (c t) -> p c t", c=KC)).then_inc(s_onhi, 1)
                act.wait_ge(s_ve, b + 1)
                link.link(nc.scalar.activation(cols[:, 1:2], cols[:, 0:1], ACT.Ln))
                nc.scalar.activation(cols[:, 2:3], cols[:, 1:2], ACT.Exp, scale=-0.5).then_inc(s_rv, 1)
                act.wait_ge(s_x1, b + 1)
                nc.scalar.activation(sq[:], x1[:], ACT.Square, accum_out=cols[:, 4:5]).then_inc(s_ms, 1)
                act.wait_ge(s_ve2, b + 1)
                link.link(nc.scalar.activation(cols[:, 6:7], cols[:, 5:6], ACT.Ln))
                nc.scalar.activation(cols[:, 7:8], cols[:, 6:7], ACT.Exp, scale=-0.5).then_inc(s_rv2, 1)
                act.wait_ge(s_xnT, b + 1)
                nc.scalar.copy(xnT[0][:, :, bass.ds(b * T, T)],
                               TB[:].rearrange("p (c t) -> p c t", c=KC)).then_inc(s_xnhi, 1)
                assert link.n == ACT_CHAIN

        @block.vector
        def _(dve):
            dve.wait_ge(s_whi, 1)
            nc.vector.tensor_tensor(w[1][:], w_raw[:], f32(w[0][:]), ALU.subtract)
            nc.vector.tensor_tensor(wo[1][:], wo_raw[:], f32(wo[0][:]), ALU.subtract).then_inc(s_wlo, 1)
            dve.wait_ge(s_const, 64)
            dve.wait_ge(s_fill, 1)
            with dve.Fori(0, B) as b:
                link = Chain(dve, c_dve, b * DVE_CHAIN)
                dve.wait_ge(s_xhi, b + 1)
                nc.vector.tensor_tensor(xT[1][:], xT_raw[:], f32(xT[0][:]), ALU.subtract).then_inc(s_xlo, 1)
                dve.wait_ge(s_qkv, b + 1)
                half = DH1 // 2
                for ps, lo, n, tab in ((Q, 0, D, 0), (KV, D, KV1, 2)):
                    src = ps[:, 0:n].rearrange("p (h d) -> p h d", d=DH1)
                    ra = rot_a[:, lo:lo + n].rearrange("p (h d) -> p h d", d=DH1)
                    rb = rot_b[:, lo:lo + n].rearrange("p (h d) -> p h d", d=DH1)
                    nh = n // DH1

                    def table(i, x, y):
                        return rope[:, tab + i:tab + i + 1, x:y].broadcast_to([P, nh, y - x])
                    nc.vector.tensor_tensor(ra, src, table(0, 0, DH1), ALU.mult)
                    nc.vector.tensor_tensor(rb[:, :, 0:half], src[:, :, half:DH1], table(1, 0, half), ALU.mult)
                    last = nc.vector.tensor_tensor(rb[:, :, half:DH1], src[:, :, 0:half], table(1, half, DH1), ALU.mult)
                nc.vector.tensor_copy(v1[:, :, 0:DH1], KV[:, KV1:2 * KV1].rearrange("p (g d) -> p g d", d=DH1))\
                    .then_inc(s_v1, 1)
                link.link(last)
                nc.vector.tensor_tensor(rot[:], rot_a[:], rot_b[:], ALU.add).then_inc(s_rot, 1)
                dve.wait_ge(s_hi3, b + 1)
                rq = rot[:, 0:D].rearrange("p (h d) -> p h d", d=DH1)
                rk = rot[:, D:D + KV1].rearrange("p (g d) -> p g d", d=DH1)
                nc.vector.tensor_tensor(q3[:, :, 2 * DH1:3 * DH1], rq, q3[:, :, 0:DH1], ALU.subtract)
                nc.vector.tensor_copy(k3[:, :, 0, 2 * DH1:3 * DH1], k3[:, :, 0, 0:DH1])
                link.link(nc.vector.tensor_tensor(k3[:, :, 0, DH1:2 * DH1], rk, k3[:, :, 0, 0:DH1], ALU.subtract))
                nc.vector.tensor_copy(k3[:, :, 1, 0:3 * DH1], k3[:, :, 0, 0:3 * DH1]).then_inc(s_lo3, 1)
                for m in range(2):
                    dve.wait_ge(s_t3, 6 * b + 5 + m)
                    src = tb[m % 2][:].rearrange("p (g t) -> p g t", g=4)
                    nc.vector.tensor_copy(k3T[0:STK, 4 * m:4 * m + 4, 0:T], src[0:STK])
                    nc.vector.tensor_copy(k3T[STK:P, 4 * m:4 * m + 4, T:2 * T], src[STK:P]).then_inc(s_k3T, 1)

                def masked_scores(j):
                    n = b * G1 + j
                    dve.wait_ge(s_s, n + 1)
                    if j >= 2:
                        dve.wait_ge(s_p, n - 1)
                    gate(nc, spare[:])
                    for r in range(R1):
                        ins = nc.vector.tensor_tensor_reduce(sm[:, j % 2, r], s_bank[j % 2][:, r * T:(r + 1) * T],
                                                             causal[:], 1.0, MASKED, ALU.add, ALU.max,
                                                             mx[:, j % 2, r:r + 1])
                    link.link(ins)
                    nc.vector.tensor_scalar(nmx[:, j % 2], mx[:, j % 2], -1.0, None, ALU.mult).then_inc(s_nm, 1)

                masked_scores(0)
                masked_scores(1)
                for j in range(G1):
                    n = b * G1 + j
                    dve.wait_ge(s_pt, n + 1)
                    if j >= 2:
                        dve.wait_ge(s_pv, n - 1)
                    nc.vector.tensor_copy(prT[:, j % 2], PT[:].rearrange("p (r t) -> p r t", r=R1)).then_inc(s_ptc, 1)
                    if j + 2 < G1:
                        masked_scores(j + 2)
                dve.wait_ge(s_pv, G1 * b + G1)
                hb = H1 // 2
                for i in range(2):
                    o = o_bank[i][:, 0:hb * (DH1 + 1)].rearrange("p (h d) -> p h d", d=DH1 + 1)
                    ins = nc.vector.reciprocal(rs[:, i * hb:(i + 1) * hb], o[:, :, DH1])
                link.link(ins)
                for i in range(2):
                    o = o_bank[i][:, 0:hb * (DH1 + 1)].rearrange("p (h d) -> p h d", d=DH1 + 1)
                    ins = nc.vector.tensor_tensor(on[:, i * hb:(i + 1) * hb, :], o[:, :, 0:DH1],
                                                  rs[:, i * hb:(i + 1) * hb].rearrange("p (h one) -> p h one", one=1)
                                                  .broadcast_to([P, hb, DH1]), ALU.mult)
                ins.then_inc(s_on, 1)
                dve.wait_ge(s_onhi, b + 1)
                nc.vector.tensor_tensor(onT[1][:], TA[:].rearrange("p (c t) -> p c t", c=KC), f32(onT[0][:]),
                                        ALU.subtract).then_inc(s_onlo, 1)
                dve.wait_ge(s_y, b + 1)
                link.link(nc.vector.tensor_tensor(y[:], Q[:], x_tok[:], ALU.add))
                link.link(nc.vector.bn_stats(st[:], y[:]))
                gate(nc, spare[:])
                link.link(nc.vector.bn_aggr(mv[:], st[:]))
                nc.vector.tensor_scalar(cols[:, 0:1], mv[:, 1:2], LN_EPS, None, ALU.add).then_inc(s_ve, 1)
                dve.wait_ge(s_rv, b + 1)
                newton(nc, link, cols[:, 0:1], cols[:, 2:3], cols[:, 3:4])
                link.link(nc.vector.tensor_scalar(x1[:], y[:], mv[:, 0:1], cols[:, 2:3], ALU.subtract, ALU.mult))
                nc.vector.tensor_scalar(acc[:, bass.ds(b, 1), :].rearrange("p b d -> p (b d)"), x1[:], 2.0, None,
                                        ALU.mult).then_inc(s_x1, 1)
                dve.wait_ge(s_ms, b + 1)
                nc.vector.tensor_scalar(cols[:, 5:6], cols[:, 4:5], 1.0 / D, LN_EPS, ALU.mult, ALU.add)\
                    .then_inc(s_ve2, 1)
                dve.wait_ge(s_rv2, b + 1)
                newton(nc, link, cols[:, 5:6], cols[:, 7:8], cols[:, 3:4])
                nc.vector.scalar_tensor_tensor(out=xn[:], in0=x1[:], scalar=cols[:, 7:8], in1=lnw[:],
                                               op0=ALU.mult, op1=ALU.mult).then_inc(s_xn, 1)
                dve.wait_ge(s_xnhi, b + 1)
                nc.vector.tensor_tensor(xnT[1][:, :, bass.ds(b * T, T)], TB[:].rearrange("p (c t) -> p c t", c=KC),
                                        f32(xnT[0][:, :, bass.ds(b * T, T)]), ALU.subtract).then_inc(s_xnlo, 1)
                assert link.n == DVE_CHAIN, link.n

        @block.tensor
        def _(pe):
            pe.wait_ge(s_wlo, 1)
            pe.wait_ge(s_const, 64)
            pe.wait_ge(s_fill, 1)
            with pe.Fori(0, B) as b:
                pe.wait_ge(s_xlo, b + 1)
                product(nc, Q[:], [[(xT[i][:, c, :], w[k][:, c, 0:D]) for c in range(KC)] for i, k in PARTS])
                product(nc, KV[:, 0:2 * KV1],
                        [[(xT[i][:, c, :], w[k][:, c, D:]) for c in range(KC)] for i, k in PARTS]).then_inc(s_qkv, 1)
                pe.wait_ge(s_lo3, b + 1)
                for m in range(6):
                    if 2 <= m < 5:
                        pe.wait_ge(s_q3T, 4 * b + m - 1)
                    if m == 5:
                        pe.wait_ge(s_q3T, 4 * b + 4)
                    for k in range(4):
                        blk = q3[:, 8 * m + 2 * k:8 * m + 2 * k + 2, :].rearrange("p h s -> p (h s)") if m < 4 else \
                            k3[:, 4 * (m - 4) + k].rearrange("p two s -> p (two s)")
                        ins = nc.tensor.transpose(tb[m % 2][:, k * T:(k + 1) * T], blk, ident[:])
                    ins.then_inc(s_t3, 1)
                pe.wait_ge(s_k3T, 2 * b + 2)
                pe.wait_ge(s_v1, b + 1)

                def scores(j):
                    if j >= 2:
                        pe.wait_ge(s_nm, G1 * b + j - 1)
                    for k in range(2):
                        ins = nc.tensor.matmul(s_bank[j % 2][:, 2 * k * T:2 * (k + 1) * T], q3T[:, 2 * j + k, :],
                                               k3T[:, j, :], start=True, stop=True)
                    ins.then_inc(s_s, 1)

                scores(0)
                scores(1)
                for j in range(G1):
                    n = b * G1 + j
                    pe.wait_ge(s_p, n + 1)
                    for r in range(R1):
                        ins = nc.tensor.transpose(PT[:, r * T:(r + 1) * T], pr[:, j % 2, r], ident[:])
                    ins.then_inc(s_pt, 1)
                    if j + 2 < G1:
                        scores(j + 2)
                    pe.wait_ge(s_ptc, n + 1)
                    for r in range(R1):
                        h = R1 * j + r
                        o = o_bank[h // (H1 // 2)]
                        col = (h % (H1 // 2)) * (DH1 + 1)
                        ins = nc.tensor.matmul(o[:, col:col + DH1 + 1], prT[:, j % 2, r], v1[:, j, :],
                                               start=True, stop=True)
                    ins.then_inc(s_pv, 1)
                pe.wait_ge(s_on, b + 1)
                for c in range(KC):
                    ins = nc.tensor.transpose(TA[:, c * T:(c + 1) * T],
                                              on[:, 8 * c:8 * c + 8, :].rearrange("p h d -> p (h d)"), ident[:])
                ins.then_inc(s_onT, 1)
                pe.wait_ge(s_onlo, b + 1)
                product(nc, Q[:], [[(onT[i][:, c, :], wo[k][:, c, :]) for c in range(KC)] for i, k in PARTS])\
                    .then_inc(s_y, 1)
                pe.wait_ge(s_xn, b + 1)
                for c in range(KC):
                    ins = nc.tensor.transpose(TB[:, c * T:(c + 1) * T], xn[:, c * P:(c + 1) * P], ident[:])
                ins.then_inc(s_xnT, 1)


def newton(nc, link, v, r, t):
    link.link(nc.vector.tensor_tensor(t, r, r, ALU.mult))
    link.link(nc.vector.tensor_tensor(t, t, v, ALU.mult))
    link.link(nc.vector.tensor_scalar(t, t, -0.5, 1.5, ALU.mult, ALU.add))
    link.link(nc.vector.tensor_tensor(r, r, t, ALU.mult))


def product(nc, out, parts, start=True):
    pairs = [p for part in parts for p in part]
    for i, (lhs, rhs) in enumerate(pairs):
        ins = nc.tensor.matmul(out, lhs, rhs, start=start and i == 0, stop=i == len(pairs) - 1)
    return ins


def cross_attention(nc, a, whole, sb, sem, banks, xnT, acc, ident, spare):
    with ExitStack() as ctx:
        cT_raw = sb(ctx, "cT_raw", [P, KC, T])
        cT = [sb(ctx, f"cT_{s}", [P, KC, B * T], F32R) for s in ("hi", "lo")]
        mask8 = sb(ctx, "mask8", [P, B, T], U8)
        mask = sb(ctx, "mask", [P, B, T])
        qk_raw = [sb(ctx, f"qk_raw{i}", [P, 2, KC, P]) for i in range(HG)]
        v_raw = sb(ctx, "v_raw", [P, KC, HG * DH2])
        o_raw = sb(ctx, "o_raw", [P, HG, D])
        wqk = [[sb(ctx, f"wqk{i}_{s}", [P, 2, KC, P], F32R) for s in ("hi", "lo")] for i in range(HG)]
        wv = [sb(ctx, f"wv_{s}", [P, KC, HG * DH2], F32R) for s in ("hi", "lo")]
        wo = [sb(ctx, f"wo_{s}", [P, HG, D], F32R) for s in ("hi", "lo")]
        bias = sb(ctx, "bias", [P, HG, T])
        bm = sb(ctx, "bm", [P, 2, HALF, T])
        qT = sb(ctx, "qT", [P, 2, HALF * T])
        kT = sb(ctx, "kT", [P, 2, HALF * T])
        v = sb(ctx, "v", [P, B, HG * DH2])
        sm = sb(ctx, "sm", [P, 2, HALF, T])
        pr = sb(ctx, "pr", [P, 2, HALF, T])
        prT = sb(ctx, "prT", [P, HALF, T])
        mx = sb(ctx, "mx", [P, 2, HALF])
        nmx = sb(ctx, "nmx", [P, 2, HALF])
        sums = sb(ctx, "sums", [P, 2, HALF])
        rsum = sb(ctx, "rsum", [P, 2, HALF])
        at = [sb(ctx, f"at_{s}", [P, 2, HG, HALF * T], F32R) for s in ("hi", "lo")]

        S = banks[0:2]
        PQ, PK, PT, PO = banks[2:6]
        PX = banks[6:8]

        s_mask_in, s_c_in = sem("b_mask_in"), sem("b_ctx_in")
        s_chi, s_clo = sem("b_ctx_hi"), sem("b_ctx_lo")
        s_mask = sem("b_mask")
        s_qk_in = [sem(f"b_qk{i}_in") for i in range(HG)]
        s_v_in, s_o_in, s_bias_in = sem("b_v_in"), sem("b_o_in"), sem("b_bias_in")
        s_wqk_h = [sem(f"b_wqk{i}_hi") for i in range(HG)]
        s_wqk = [sem(f"b_wqk{i}") for i in range(HG)]
        s_wv_h, s_wv = sem("b_wv_hi"), sem("b_wv")
        s_wo_h, s_wo = sem("b_wo_hi"), sem("b_wo")
        s_bm = sem("b_bias_mask")
        s_q, s_k, s_qT, s_kT = sem("b_q"), sem("b_k"), sem("b_qT"), sem("b_kT")
        s_v, s_vc = sem("b_v"), sem("b_v_copied")
        s_s, s_nm, s_e, s_p = sem("b_scores"), sem("b_negmax"), sem("b_exp"), sem("b_probs")
        s_t, s_prT, s_pv = sem("b_probs_transposed"), sem("b_prT"), sem("b_pv")
        s_ah, s_al = sem("b_at_hi"), sem("b_at_lo")
        s_out, s_acc = sem("b_out"), sem("b_acc")
        c_dve = sem("b_dve_chain")
        DVE_CHAIN = 3

        block = ctx.enter_context(nc.Block())

        def one(ap, g):
            return ap[bass.ds(g, 1)]

        def groups(eng, step):
            step(0, True, False)
            with eng.Fori(1, NG - 1) as g:
                step(g, False, False)
            step(NG - 1, False, True)

        def old_out(g, s, first):
            if first:
                return None
            return (B * (g - 1), B * (g - 1) + HALF, B * (g - 1) + HALF, B * g)[s]

        @block.sync
        def _(sp):
            def load_qk(i, g):
                sp.dma_start(qk_raw[i][:], one(a["wqk"], g)[:, :, i].rearrange("g p q c j -> p (g q) c j"))\
                    .then_inc(s_qk_in[i], 16)

            def load_v(g):
                sp.dma_start(v_raw[:], one(a["wv"], g).rearrange("g p c j -> p (g c) j")).then_inc(s_v_in, 16)

            def load_o(g):
                sp.dma_start(o_raw[:], one(a["wo"], g).rearrange("g p i n -> p (g i) n")).then_inc(s_o_in, 16)

            def load_bias(g):
                sp.dma_start(bias[:], one(a["bias"], g).rearrange("g p i k -> p (g i) k")).then_inc(s_bias_in, 16)

            load_qk(0, 0)
            load_v(0)
            load_qk(1, 0)
            sp.dma_start(mask8[:], a["mask"]).then_inc(s_mask_in, 16)
            load_bias(0)
            load_o(0)
            with sp.Fori(0, B) as b:
                sp.wait_ge(s_clo, b)
                sp.dma_start(cT_raw[:], a["cT"][bass.ds(b, 1)].rearrange("b p c t -> p (b c) t")).then_inc(s_c_in, 16)

            with sp.Fori(0, NG - 1) as g:
                sp.wait_ge(s_wv, g + 1)
                load_v(g + 1)
                sp.wait_ge(s_wqk[0], g + 1)
                load_qk(0, g + 1)
                sp.wait_ge(s_wqk[1], g + 1)
                load_qk(1, g + 1)
                sp.wait_ge(s_wo, g + 1)
                load_o(g + 1)
                sp.wait_ge(s_bm, TILES * g + TILES)
                load_bias(g + 1)

        @block.gpsimd
        def _(pool):
            def bias_mask(g, s, first):
                n = TILES * g + s
                if s == 0:
                    pool.wait_ge(s_bias_in, 16 * g + 16)
                if not first or s >= 2:
                    pool.wait_ge(s_nm, n - 1)
                nc.gpsimd.tensor_tensor(bm[:, s % 2], mask[:, HALF * (s // HG):HALF * (s // HG + 1), :],
                                        bias[:, s % HG:s % HG + 1, :].broadcast_to([P, HALF, T]), ALU.add)\
                    .then_inc(s_bm, 1)

            pool.wait_ge(s_mask, 1)
            for s in range(TILES):
                bias_mask(0, s, True)
            with pool.Fori(1, NG) as g:
                for s in range(TILES):
                    bias_mask(g, s, False)

        @block.scalar
        def _(act):
            def hi_qk(i, g, first=False):
                act.wait_ge(s_qk_in[i], 16 * g + 16)
                if not first:
                    act.wait_ge(s_k, TILES * g - 1 + i)
                nc.scalar.copy(wqk[i][0][:], qk_raw[i][:]).then_inc(s_wqk_h[i], 1)

            def hi_v(g, first=False):
                act.wait_ge(s_v_in, 16 * g + 16)
                if not first:
                    act.wait_ge(s_v, B * g)
                nc.scalar.copy(wv[0][:], v_raw[:]).then_inc(s_wv_h, 1)

            def hi_o(g, first):
                act.wait_ge(s_o_in, 16 * g + 16)
                if not first:
                    act.wait_ge(s_out, B * g)
                nc.scalar.copy(wo[0][:], o_raw[:]).then_inc(s_wo_h, 1)

            def copy_qk(n, m):
                act.wait_ge(s_q, n + 1)
                nc.scalar.copy(qT[:, m % 2], PQ[:]).then_inc(s_qT, 1)
                act.wait_ge(s_k, n + 1)
                nc.scalar.copy(kT[:, m % 2], PK[:]).then_inc(s_kT, 1)

            def copy_v(c, b, used):
                act.wait_ge(s_v, c + 1)
                if used is not None:
                    act.wait_ge(s_pv, used)
                nc.scalar.copy(v[:, b, :], PX[b % 2][:, 0:HG * DH2]).then_inc(s_vc, 1)

            def exps(n, s, first):
                act.wait_ge(s_nm, n + 1)
                if not first or s >= 2:
                    act.wait_ge(s_t, n - 1)
                for k in range(HALF):
                    e = nc.scalar.activation(pr[:, s % 2, k], sm[:, s % 2, k], ACT.Exp,
                                             bias=nmx[:, s % 2, k:k + 1], accum_out=sums[:, s % 2, k:k + 1])
                e.then_inc(s_e, 1)

            def copy_prT(n, first):
                act.wait_ge(s_t, n + 1)
                if not first:
                    act.wait_ge(s_pv, n)
                nc.scalar.copy(prT[:], PT[:].rearrange("p (b t) -> p b t", b=HALF)).then_inc(s_prT, 1)

            def at_hi(n, s, used):
                act.wait_ge(s_pv, n + 1)
                if used is not None:
                    act.wait_ge(s_out, used)
                nc.scalar.copy(at[0][:, s // HG, s % HG], PO[:]).then_inc(s_ah, 1)

            def step(g, first, last):
                for s in range(TILES):
                    n = TILES * g + s
                    if s == 2:
                        if not last:
                            hi_v(g + 1)
                        hi_o(g, first)
                        if not last:
                            hi_qk(0, g + 1)
                    if s == 3 and not last:
                        hi_qk(1, g + 1)
                    exps(n, s, first)
                    if not (last and s == TILES - 1):
                        copy_qk(n + 1, s + 1)
                    prev = not (first and s == 0)
                    if prev:
                        copy_prT(n - 1, first and s == 1)
                    b = (HALF + 2 * s) % B
                    has_v = not (last and s >= 2)
                    used = (None if first else TILES * g) if s < 2 else TILES * g + 2
                    if has_v:
                        copy_v(2 * n + HALF, b, used)
                    if prev:
                        at_hi(n - 1, (s - 1) % TILES, old_out(g, s, first))
                    if has_v:
                        copy_v(2 * n + HALF + 1, b + 1, used)
                if last:
                    n = TILES * NG
                    copy_prT(n - 1, False)
                    at_hi(n - 1, TILES - 1, B * (NG - 1))

            with act.Fori(0, B) as b:
                act.wait_ge(s_c_in, 16 * b + 16)
                nc.scalar.copy(cT[0][:, :, bass.ds(b * T, T)], cT_raw[:]).then_inc(s_chi, 1)
            hi_qk(0, 0, True)
            hi_v(0, True)
            hi_qk(1, 0, True)
            copy_qk(0, 0)
            for b in range(HALF):
                copy_v(b, b, None)
            groups(act, step)

        @block.vector
        def _(dve):
            def lo(parts, raw, s_h, s_done, count):
                dve.wait_ge(s_h, count)
                nc.vector.tensor_tensor(parts[1][:], raw[:], f32(parts[0][:]), ALU.subtract).then_inc(s_done, 1)

            def masked_scores(n, s, first, link):
                dve.wait_ge(s_s, n + 1)
                dve.wait_ge(s_bm, n + 1)
                if not first or s >= 2:
                    dve.wait_ge(s_e, n - 1)
                gate(nc, spare[:])
                for k in range(HALF):
                    ins = nc.vector.tensor_tensor_reduce(sm[:, s % 2, k], S[s % 2][:, k * T:(k + 1) * T],
                                                         bm[:, s % 2, k], 1.0, FLOOR, ALU.add, ALU.max,
                                                         mx[:, s % 2, k:k + 1])
                link.link(ins)
                nc.vector.tensor_scalar(nmx[:, s % 2], mx[:, s % 2], -1.0, None, ALU.mult).then_inc(s_nm, 1)

            def normalise(n, s, link):
                dve.wait_ge(s_e, n + 1)
                link.link(nc.vector.tensor_scalar(rsum[:, s % 2], sums[:, s % 2], 0.5, None, ALU.max))
                link.link(nc.vector.reciprocal(rsum[:, s % 2], rsum[:, s % 2]))
                nc.vector.tensor_tensor(pr[:, s % 2], pr[:, s % 2],
                                        rsum[:, s % 2].rearrange("p (b one) -> p b one", one=1)
                                        .broadcast_to([P, HALF, T]), ALU.mult).then_inc(s_p, 1)

            def at_lo(n, s):
                dve.wait_ge(s_ah, n + 1)
                nc.vector.tensor_tensor(at[1][:, s // HG, s % HG], PO[:], f32(at[0][:, s // HG, s % HG]),
                                        ALU.subtract).then_inc(s_al, 1)

            def accumulate(n, j, b):
                dve.wait_ge(s_out, 2 * n - HALF + j + 1)
                dve.wait_ge(s_acc, 2 * n - HALF)
                nc.vector.tensor_tensor(acc[:, b], acc[:, b], PX[b % 2][:], ALU.add).then_inc(s_acc, 1)

            def step(g, first, last):
                for s in range(TILES):
                    n = TILES * g + s
                    link = Chain(dve, c_dve, DVE_CHAIN * n)
                    if s == 2 and not last:
                        lo(wv, v_raw, s_wv_h, s_wv, g + 2)
                    if s == 2:
                        lo(wo, o_raw, s_wo_h, s_wo, g + 1)
                    masked_scores(n, s, first, link)
                    if s == 2 and not last:
                        lo(wqk[0], qk_raw[0], s_wqk_h[0], s_wqk[0], g + 2)
                    if s == 3 and not last:
                        lo(wqk[1], qk_raw[1], s_wqk_h[1], s_wqk[1], g + 2)
                    normalise(n, s, link)
                    assert link.n == DVE_CHAIN
                    if not (first and s == 0):
                        at_lo(n - 1, (s - 1) % TILES)
                    if not (first and s < 2):
                        for j in range(2):
                            accumulate(n, j, (HALF + 2 * s + j) % B)
                if last:
                    n = TILES * NG
                    at_lo(n - 1, TILES - 1)
                    for j in range(HALF):
                        accumulate(n, j, HALF + j)

            dve.wait_ge(s_mask_in, 16)
            nc.vector.tensor_scalar(mask[:], mask8[:], -1.0, -MASKED, ALU.add, ALU.mult).then_inc(s_mask, 1)
            with dve.Fori(0, B) as b:
                dve.wait_ge(s_chi, b + 1)
                nc.vector.tensor_tensor(cT[1][:, :, bass.ds(b * T, T)], cT_raw[:],
                                        f32(cT[0][:, :, bass.ds(b * T, T)]), ALU.subtract).then_inc(s_clo, 1)
            lo(wqk[0], qk_raw[0], s_wqk_h[0], s_wqk[0], 1)
            lo(wv, v_raw, s_wv_h, s_wv, 1)
            lo(wqk[1], qk_raw[1], s_wqk_h[1], s_wqk[1], 1)
            groups(dve, step)

        @block.tensor
        def _(pe):
            def project_qk(g, m):
                i, half = m % HG, m // HG
                tok = slice(half * HALF * T, (half + 1) * HALF * T)
                pe.wait_ge(s_wqk[i], g + 1)
                product(nc, PQ[:], [[(wqk[i][p][:, 0, c], xnT[q][:, c, tok]) for c in range(KC)] for p, q in PARTS])\
                    .then_inc(s_q, 1)
                product(nc, PK[:], [[(wqk[i][p][:, 1, c], cT[q][:, c, tok]) for c in range(KC)] for p, q in PARTS])\
                    .then_inc(s_k, 1)

            def project_v(b):
                product(nc, PX[b % 2][:, 0:HG * DH2],
                        [[(cT[p][:, c, b * T:(b + 1) * T], wv[q][:, c, :]) for c in range(KC)] for p, q in PARTS])\
                    .then_inc(s_v, 1)

            def scores(n, s, first):
                pe.wait_ge(s_kT, n + 1)
                if not first or s >= 2:
                    pe.wait_ge(s_nm, n - 1)
                for k in range(HALF):
                    tok = slice(k * T, (k + 1) * T)
                    ins = nc.tensor.matmul(S[s % 2][:, tok], qT[:, s % 2, tok], kT[:, s % 2, tok],
                                           start=True, stop=True)
                ins.then_inc(s_s, 1)

            def transposes(n, s):
                pe.wait_ge(s_p, n + 1)
                for k in range(HALF):
                    ins = nc.tensor.transpose(PT[:, k * T:(k + 1) * T], pr[:, s % 2, k], ident[:])
                ins.then_inc(s_t, 1)

            def pv(n, s, v_ready, first):
                pe.wait_ge(s_prT, n + 1)
                pe.wait_ge(s_vc, v_ready)
                if not first:
                    pe.wait_ge(s_al, n)
                half, i = s // HG, s % HG
                for k in range(HALF):
                    ins = nc.tensor.matmul(PO[:, k * T:(k + 1) * T], v[:, half * HALF + k, i * DH2:(i + 1) * DH2],
                                           prT[:, k], start=True, stop=True)
                ins.then_inc(s_pv, 1)

            def output(b, half):
                tok = slice((b - half * HALF) * T, (b - half * HALF + 1) * T)
                product(nc, PX[b % 2][:], [[(at[p][:, half, i, tok], wo[q][:, i, :]) for i in range(HG)]
                                           for p, q in PARTS]).then_inc(s_out, 1)

            def step(g, first, last):
                for s in range(TILES):
                    n = TILES * g + s
                    prev, sp = not (first and s == 0), (s - 1) % TILES
                    has_v = not (last and s >= 2)
                    had_out = not (first and s < 3)
                    scores(n, s, first)
                    if not (last and s == TILES - 1):
                        project_qk(g if s < TILES - 1 else g + 1, (s + 1) % TILES)
                    if prev:
                        transposes(n - 1, sp)
                    for j in range(2):
                        if has_v:
                            b = (HALF + 2 * s + j) % B
                            pe.wait_ge(s_wv, g + 1 if s < 2 else g + 2)
                            if had_out:
                                pe.wait_ge(s_acc, 2 * n - 5 + j)
                            pe.wait_ge(s_vc, 2 * n + 3 + j)
                            project_v(b)
                        if j == 0 and prev:
                            v_ready = B * g if s == 0 else B * g + HALF * (sp // HG + 1)
                            pv(n - 1, sp, v_ready, first and s == 1)
                    if not (first and s < 2):
                        half = 0 if s >= 2 else 1
                        if s in (0, 2):
                            pe.wait_ge(s_al, n)
                        if s == 2:
                            pe.wait_ge(s_wo, g + 1)
                        for j in range(2):
                            if has_v:
                                pe.wait_ge(s_vc, 2 * n + HALF + 1 + j)
                            else:
                                pe.wait_ge(s_acc, 2 * n - 5 + j)
                            output((HALF + 2 * s + j) % B, half)
                if last:
                    n = TILES * NG
                    transposes(n - 1, TILES - 1)
                    pv(n - 1, TILES - 1, B * NG, False)
                    pe.wait_ge(s_al, n)
                    for j in range(HALF):
                        pe.wait_ge(s_acc, 2 * n - 5 + j)
                        output(HALF + j, 1)

            pe.wait_ge(s_clo, B)
            project_qk(0, 0)
            pe.wait_ge(s_wv, 1)
            for b in range(HALF):
                if b >= 2:
                    pe.wait_ge(s_vc, b - 1)
                project_v(b)
            groups(pe, step)


def experts(nc, a, whole, sb, sem, banks, acc, ident, spare, out_d):
    with ExitStack() as ctx:
        wb_raw = sb(ctx, "wb_raw", [P, KC, D])
        wb = [sb(ctx, f"wb_{s}", [P, KC, D], F32R) for s in ("hi", "lo")]
        war = sb(ctx, "war", [P, KC, E * RK + E])
        wB = sb(ctx, "wB", [P, D])
        b_base = sb(ctx, "b_base", [P, D])
        router_b = sb(ctx, "router_b", [P, E])
        prior = sb(ctx, "prior", [P, E])
        active = sb(ctx, "active", [P, EA], I32)
        active_f = sb(ctx, "active_f", [P, EA])
        iota = sb(ctx, "iota", [P, E])
        hit = sb(ctx, "hit", [P, E])
        count = sb(ctx, "count", [P, E])
        logit0 = sb(ctx, "logit0", [P, E])
        x2 = sb(ctx, "x2", [P, D])
        x2T_f = sb(ctx, "x2T_f", [P, KC, T])
        x2T = [sb(ctx, f"x2T_{s}", [P, KC, T], F32R) for s in ("hi", "lo")]
        logit = sb(ctx, "logit", [P, E])
        alpha = sb(ctx, "alpha", [P, E])
        u = sb(ctx, "u", [P, E, RK])
        uT = sb(ctx, "uT", [P, T])
        y = sb(ctx, "y2", [P, D])
        o = sb(ctx, "o2", [P, D])
        st = sb(ctx, "st2", [P, 6])
        mv = sb(ctx, "mv2", [P, 2])
        cols = sb(ctx, "cols2", [P, 8])
        XT, BASE, AR, UT = banks[0:4]

        s_in = sem("c_in")
        s_whi, s_wlo = sem("c_w_hi"), sem("c_w_lo")
        s_lp = sem("c_log_prior")
        s_pe_, s_ve, s_rv = sem("c_prior_eps"), sem("c_var"), sem("c_rstd_guess")
        s_x2, s_xt, s_xf, s_xh, s_xl = (sem("c_" + n) for n in ("x2", "x2_transposed", "x2T", "x2T_hi", "x2T_lo"))
        s_ar, s_base, s_lg, s_al, s_u, s_ut, s_utc, s_mm = (sem("c_" + n) for n in (
            "experts_a", "base", "logits", "alpha_exp", "u", "u_transposed", "uT", "sum"))
        s_ve2, s_rv2, s_o, s_st = sem("c_var2"), sem("c_rstd_guess2"), sem("c_o"), sem("c_stored")
        c_act, c_dve, c_pre = sem("c_act_chain"), sem("c_dve_chain"), sem("c_pre_chain")
        ACT_CHAIN, DVE_CHAIN = 2, 19

        block = ctx.enter_context(nc.Block())

        @block.sync
        def _(sp):
            sp.dma_start(wb_raw[:], a["wbase"]).then_inc(s_in, 16)
            sp.dma_start(war[:], a["war"]).then_inc(s_in, 16)
            sp.dma_start(wB[:], a["wB"]).then_inc(s_in, 16)
            sp.dma_start(b_base[:], a["b_base"].partition_broadcast(P)).then_inc(s_in, 16)
            sp.dma_start(router_b[:], a["router_b"].partition_broadcast(P)).then_inc(s_in, 16)
            sp.dma_start(prior[:], a["prior"].partition_broadcast(P)).then_inc(s_in, 16)
            sp.dma_start(active[:], a["active"].partition_broadcast(P)).then_inc(s_in, 16)
            sp.dma_start(iota[:], a["iota"].partition_broadcast(P)).then_inc(s_in, 16)
            with sp.Fori(0, B) as b:
                sp.wait_ge(s_o, b + 1)
                sp.dma_start(out_d[bass.ds(b * T, T), :], o[:]).then_inc(s_st, 16)
            sp.wait_ge(s_st, 16 * B)

        @block.scalar
        def _(act):
            act.wait_ge(s_in, 128)
            nc.scalar.copy(wb[0][:], wb_raw[:]).then_inc(s_whi, 1)
            act.wait_ge(s_pe_, 1)
            nc.scalar.activation(logit0[:], hit[:], ACT.Ln).then_inc(s_lp, 1)
            with act.Fori(0, B) as b:
                link = Chain(act, c_act, b * ACT_CHAIN)
                act.wait_ge(s_ve, b + 1)
                link.link(nc.scalar.activation(cols[:, 1:2], cols[:, 0:1], ACT.Ln))
                nc.scalar.activation(cols[:, 2:3], cols[:, 1:2], ACT.Exp, scale=-0.5).then_inc(s_rv, 1)
                act.wait_ge(s_xt, b + 1)
                nc.scalar.copy(x2T_f[:], XT[:].rearrange("p (c t) -> p c t", c=KC)).then_inc(s_xf, 1)
                nc.scalar.copy(x2T[0][:], XT[:].rearrange("p (c t) -> p c t", c=KC)).then_inc(s_xh, 1)
                act.wait_ge(s_lg, b + 1)
                nc.scalar.activation(alpha[:], logit[:], ACT.Exp, bias=cols[:, 4:5]).then_inc(s_al, 1)
                act.wait_ge(s_ut, b + 1)
                nc.scalar.copy(uT[:], UT[:, 0:T]).then_inc(s_utc, 1)
                act.wait_ge(s_ve2, b + 1)
                link.link(nc.scalar.activation(cols[:, 1:2], cols[:, 0:1], ACT.Ln))
                nc.scalar.activation(cols[:, 2:3], cols[:, 1:2], ACT.Exp, scale=-0.5).then_inc(s_rv2, 1)
                assert link.n == ACT_CHAIN

        @block.vector
        def _(dve):
            pre = Chain(dve, c_pre, 0)
            dve.wait_ge(s_in, 128)
            pre.link(nc.vector.tensor_copy(active_f[:], active[:]))
            pre.link(nc.vector.tensor_scalar(count[:], iota[:], active_f[:, 0:1], None, ALU.is_equal))
            for k in range(1, EA):
                pre.link(nc.vector.tensor_scalar(hit[:], iota[:], active_f[:, k:k + 1], None, ALU.is_equal))
                pre.link(nc.vector.tensor_tensor(count[:], count[:], hit[:], ALU.add))
            nc.vector.tensor_scalar(hit[:], prior[:], PRIOR_EPS, None, ALU.add).then_inc(s_pe_, 1)
            dve.wait_ge(s_lp, 1)
            pre.link(nc.vector.tensor_tensor(logit0[:], logit0[:], router_b[:], ALU.add))
            pre.link(nc.vector.tensor_scalar(hit[:], count[:], 0.0, MASKED, ALU.is_equal, ALU.mult))
            pre.link(nc.vector.tensor_tensor(logit0[:], logit0[:], hit[:], ALU.add))
            dve.wait_ge(s_whi, 1)
            nc.vector.tensor_tensor(wb[1][:], wb_raw[:], f32(wb[0][:]), ALU.subtract).then_inc(s_wlo, 1)

            def norm(link, src, dst, s_v, s_r, b):
                link.link(nc.vector.bn_stats(st[:], src))
                gate(nc, spare[:])
                link.link(nc.vector.bn_aggr(mv[:], st[:]))
                nc.vector.tensor_scalar(cols[:, 0:1], mv[:, 1:2], LN_EPS, None, ALU.add).then_inc(s_v, 1)
                dve.wait_ge(s_r, b + 1)
                newton(nc, link, cols[:, 0:1], cols[:, 2:3], cols[:, 3:4])
                return nc.vector.tensor_scalar(dst, src, mv[:, 0:1], cols[:, 2:3], ALU.subtract, ALU.mult)

            with dve.Fori(0, B) as b:
                link = Chain(dve, c_dve, b * DVE_CHAIN)
                norm(link, acc[:, bass.ds(b, 1), :].rearrange("p b d -> p (b d)"), x2[:], s_ve, s_rv, b)\
                    .then_inc(s_x2, 1)
                dve.wait_ge(s_xh, b + 1)
                nc.vector.tensor_tensor(x2T[1][:], XT[:].rearrange("p (c t) -> p c t", c=KC), f32(x2T[0][:]),
                                        ALU.subtract).then_inc(s_xl, 1)
                dve.wait_ge(s_ar, b + 1)
                link.link(nc.vector.tensor_tensor(logit[:], AR[:, E * RK:E * RK + E], logit0[:], ALU.add))
                nc.vector.tensor_reduce(cols[:, 4:5], logit[:], AX_X, ALU.max, negate=True).then_inc(s_lg, 1)
                dve.wait_ge(s_al, b + 1)
                link.link(nc.vector.tensor_tensor(alpha[:], alpha[:], count[:], ALU.mult))
                link.link(nc.vector.reduce_sum(cols[:, 5:6], alpha[:], AX_X))
                link.link(nc.vector.reciprocal(cols[:, 6:7], cols[:, 5:6]))
                link.link(nc.vector.tensor_scalar(alpha[:], alpha[:], cols[:, 6:7], SCALING, ALU.mult, ALU.mult))
                nc.vector.tensor_tensor(u[:], AR[:, 0:E * RK].rearrange("p (e r) -> p e r", r=RK),
                                        alpha[:].rearrange("p (e one) -> p e one", one=1).broadcast_to([P, E, RK]),
                                        ALU.mult).then_inc(s_u, 1)
                link.link(nc.vector.tensor_tensor(y[:], x2[:], b_base[:], ALU.add))
                dve.wait_ge(s_mm, b + 1)
                link.link(nc.vector.tensor_tensor(y[:], y[:], BASE[:], ALU.add))
                dve.wait_ge(s_st, 16 * b)
                norm(link, y[:], o[:], s_ve2, s_rv2, b).then_inc(s_o, 1)
                assert link.n == DVE_CHAIN, link.n

        @block.tensor
        def _(pe):
            pe.wait_ge(s_in, 128)
            pe.wait_ge(s_wlo, 1)
            with pe.Fori(0, B) as b:
                pe.wait_ge(s_x2, b + 1)
                for c in range(KC):
                    ins = nc.tensor.transpose(XT[:, c * T:(c + 1) * T], x2[:, c * P:(c + 1) * P], ident[:])
                ins.then_inc(s_xt, 1)
                pe.wait_ge(s_xf, b + 1)
                for c in range(KC):
                    ins = nc.tensor.matmul(AR[:, 0:E * RK + E], x2T_f[:, c, :], war[:, c, :],
                                           start=c == 0, stop=c == KC - 1)
                ins.then_inc(s_ar, 1)
                pe.wait_ge(s_xl, b + 1)
                pairs = [(x2T[i][:, c, :], wb[k][:, c, :]) for i, k in PARTS for c in range(KC)]
                for i, (lhs, rhs) in enumerate(pairs):
                    nc.tensor.matmul(BASE[:], lhs, rhs, start=i == 0, stop=False)
                pe.wait_ge(s_u, b + 1)
                nc.tensor.transpose(UT[:, 0:T], u[:].rearrange("p e r -> p (e r)"), ident[:]).then_inc(s_ut, 1)
                pe.wait_ge(s_utc, b + 1)
                nc.tensor.matmul(BASE[:], uT[:], wB[:], start=False, stop=True).then_inc(s_mm, 1)


def rope_tables():
    f = np.float32
    inv = (1.0 / np.power(f(500000.0), np.arange(0, DH1, 2, dtype=f) / f(DH1))).astype(f)
    wavelen = (f(2.0 * np.pi) / inv).astype(f)
    lo, hi = 1024 / 4.0, 1024 / 1.0
    inv2 = np.where(wavelen > hi, inv / f(32.0), inv).astype(f)
    smooth = ((f(1024) / wavelen - f(1.0)) / f(3.0)).astype(f)
    smoothed = ((f(1.0) - smooth) * inv2 / f(32.0) + smooth * inv2).astype(f)
    medium = ~(wavelen < hi) & ~(wavelen > lo)
    inv3 = np.where(medium, smoothed, inv2).astype(f)
    freqs = (np.arange(T, dtype=f)[:, None] * inv3[None, :]).astype(f)
    emb = np.concatenate([freqs, freqs], axis=-1)
    cos, sin = np.cos(emb).astype(f), np.sin(emb).astype(f)
    sin = np.concatenate([-sin[:, :DH1 // 2], sin[:, DH1 // 2:]], axis=-1)
    s = f(DH1 ** -0.5)
    return np.ascontiguousarray(np.stack([cos * s, sin * s, cos, sin], axis=1))


def kernel(x, ctx_4096, mask_BxSxS2_bk0, L0_attn_Wq, L0_attn_Wk, L0_attn_Wv, L0_attn_Wo, L0_xattn_position_bias,
           L0_xattn_ln_weight, L0_xattn_w_q, L0_xattn_w_k, L0_xattn_w_v, L0_xattn_w_out, L0_ffn_W_base,
           L0_ffn_b_base, L0_ffn_lora_A, L0_ffn_lora_B, L0_ffn_router_W, L0_ffn_router_b, L0_ffn_domain_prior,
           L0_ffn_active):
    import concourse.bacc as bacc
    from concourse.bass_utils import run_bass_kernel_spmd

    def arr(v):
        return np.asarray(v)

    def chunks(wt):
        return wt.reshape(KC, P, -1).transpose(1, 0, 2)

    def tokens(v):
        return v.reshape(B, T, KC, P).transpose(0, 3, 2, 1)

    def heads(wm):
        return wm.T.reshape(KC, P, NG, HG, DH2).transpose(2, 1, 0, 3, 4)

    xa, wo2 = arr(x), arr(L0_xattn_w_out)
    wqk = np.stack([heads(arr(L0_xattn_w_q)), heads(arr(L0_xattn_w_k))], axis=0)
    tri = np.tril(np.ones((T, T), dtype=bool))
    arrays = {
        "xT": tokens(xa),
        "x": xa,
        "cT": tokens(arr(ctx_4096)),
        "wqkv1": chunks(np.concatenate([arr(L0_attn_Wq), arr(L0_attn_Wk), arr(L0_attn_Wv)], axis=0).T),
        "wo1": chunks(arr(L0_attn_Wo).T),
        "wqk": wqk.transpose(1, 2, 4, 0, 3, 5),
        "wv": heads(arr(L0_xattn_w_v)).reshape(NG, P, KC, HG * DH2),
        "wo": wo2.T.reshape(NG, HG, DH2, D).transpose(0, 2, 1, 3),
        "bias": arr(L0_xattn_position_bias).reshape(NG, HG, T, T).transpose(0, 2, 1, 3),
        "mask": arr(mask_BxSxS2_bk0).transpose(1, 0, 2),
        "lnw": arr(L0_xattn_ln_weight),
        "wbase": chunks(arr(L0_ffn_W_base).T),
        "war": chunks(np.concatenate([arr(L0_ffn_lora_A).reshape(E * RK, D), arr(L0_ffn_router_W)], axis=0).T),
        "wB": arr(L0_ffn_lora_B).transpose(0, 2, 1).reshape(E * RK, D),
        "b_base": arr(L0_ffn_b_base),
        "router_b": arr(L0_ffn_router_b),
        "prior": arr(L0_ffn_domain_prior),
        "active": arr(L0_ffn_active),
        "iota": np.arange(E, dtype=np.float32),
        "ident": np.eye(P, dtype=np.float32),
        "causal": np.where(tri, np.float32(0), np.float32(MASKED)),
        "rope": rope_tables(),
    }
    nc = bacc.Bacc("TRN2", target_bir_lowering=False, num_devices=1)
    ins, aps = {}, {}
    for name, v in arrays.items():
        ins[f"in_{name}"] = np.ascontiguousarray(v)
        aps[name] = nc.dram_tensor(f"in_{name}", v.shape, mybir.dt.from_np(v.dtype), kind="ExternalInput").ap()
    aps["out"] = nc.dram_tensor("out_0", (B, T, D), F32, kind="ExternalOutput").ap()
    build(nc, aps)
    r = run_bass_kernel_spmd(nc, [ins], core_ids=[0])
    return r.results[0]["out_0"]
```

```python
from contextlib import ExitStack

import numpy as np
import concourse.bass as bass
from concourse import mybir

ALU = mybir.AluOpType
ACT = mybir.ActivationFunctionType
AX_X = mybir.AxisListType.X
F32 = mybir.dt.float32
F32R = mybir.dt.float32r
I32 = mybir.dt.int32
U8 = mybir.dt.uint8

P = 128
B, T, D = 8, 128, 512
KC = D // P
H1, G1, DH1 = 32, 8, 16
R1 = H1 // G1
KV1 = G1 * DH1
STK = 4 * DH1
H2, DH2 = 32, 128
HG = 2
NG = H2 // HG
HALF = B // 2
TILES = 2 * HG
E, RK, EA = 16, 8, 4
LN_EPS = 1e-5
PRIOR_EPS = 1e-12
SCALING = 2.0
MASKED = -1.0e30
FLOOR = -1.0e29
PARTS = ((0, 0), (0, 1), (1, 0))


def gate(nc, spare):
    nc.vector.memset(spare, 0.0)


class Chain:

    def __init__(self, eng, sem, start):
        self.eng, self.sem, self.start, self.n = eng, sem, start, 0

    def link(self, ins):
        self.n += 1
        ins.then_inc(self.sem, 1)
        self.eng.wait_ge(self.sem, self.start + self.n)


def build(nc, a):
    out_d = a["out"].rearrange("b t d -> (b t) d")
    with ExitStack() as whole:
        def sb(ctx, name, shape, dt=F32):
            return ctx.enter_context(nc.sbuf_tensor(name, shape, dt))

        def sem(name):
            return whole.enter_context(nc.semaphore(name))

        banks = [whole.enter_context(nc.psum_tensor(f"bank{i}", [P, 512], F32)) for i in range(8)]

        xnT = [sb(whole, f"xnT_{s}", [P, KC, B * T], F32R) for s in ("hi", "lo")]
        acc = sb(whole, "acc", [P, B, D])
        stage = sb(whole, "stage", [P, KC * B * T])
        ident = sb(whole, "ident", [P, P])
        spare = sb(whole, "spare", [P, 4])

        s_stage = self_attention(nc, a, whole, sb, sem, banks, xnT, acc, stage, ident, spare)
        s_experts_in = cross_attention(nc, a, whole, sb, sem, banks, xnT, acc, stage, s_stage, ident, spare)
        experts(nc, a, whole, sb, sem, banks, acc, stage, s_experts_in, ident, spare, out_d)


def f32(ap):
    return ap.bitcast(F32)


def at_least(eng, sem, value):
    if not isinstance(value, int) or value > 0:
        eng.wait_ge(sem, value)


def live(b):
    return not isinstance(b, int) or 0 <= b < B


def steps(eng, step):
    step(0, 0)
    step(1, 1)
    with eng.Fori(1, B // 2) as pair:
        step(2 * pair, 0)
        step(2 * pair + 1, 1)
    step(B, 0)
    step(B + 1, 1)


def self_attention(nc, a, whole, sb, sem, banks, xnT, acc, stage, ident, spare):
    with ExitStack() as ctx:
        NW = D + 2 * KV1 + D
        w_raw = [sb(ctx, f"w1_raw{i}", [P, NW]) for i in range(2)]
        w = [sb(ctx, f"w1_{s}", [P, KC, NW], F32R) for s in ("hi", "lo")]
        xT_raw = sb(ctx, "xT_raw", [P, KC, T])
        xT = [sb(ctx, f"xT_{s}", [P, KC, T], F32R) for s in ("hi", "lo")]
        rope = sb(ctx, "rope", [P, 4, DH1])
        causal = sb(ctx, "causal", [P, T])
        lnw = sb(ctx, "lnw", [P, D])
        minus_half = sb(ctx, "minus_half", [P, 1])
        eps = sb(ctx, "eps", [P, 1])
        rot_a = sb(ctx, "rot_a", [P, D + KV1])
        rot_b = sb(ctx, "rot_b", [P, D + KV1])
        rot = sb(ctx, "rot", [P, D + KV1])
        q3 = sb(ctx, "q3", [P, H1, STK])
        k3 = sb(ctx, "k3", [P, G1, 2, STK])
        q3T = sb(ctx, "q3T", [P, 2, H1 // 2, T], F32R)
        k3T = sb(ctx, "k3T", [P, 2, G1, 2 * T], F32R)
        v1 = sb(ctx, "v1", [P, 2, G1, DH1 + 1])
        sm = sb(ctx, "sm1", [P, 2, R1, T])
        pr = sb(ctx, "pr1", [P, 2, R1, T])
        prT = sb(ctx, "prT1", [P, 2, R1, T])
        mx = sb(ctx, "mx1", [P, 2, R1])
        rs = sb(ctx, "rs1", [P, H1])
        on = sb(ctx, "on", [P, H1, DH1])
        onT = [sb(ctx, f"onT_{s}", [P, KC, T], F32R) for s in ("hi", "lo")]
        y = sb(ctx, "y1", [P, D])
        x1 = sb(ctx, "x1", [P, D])
        xn = sb(ctx, "xn", [P, D])
        st = sb(ctx, "st1", [P, 6])
        mv = sb(ctx, "mv1", [P, 2])
        cols = sb(ctx, "cols1", [P, 4])

        QB, KVB, TA, SA, SB_, PT, O0, O1 = banks
        tb = [TA, QB]
        s_bank = [SA, SB_]
        o_bank = [O0, O1]
        HB = H1 // 2

        s_const, s_w, s_x, s_res = sem("a_const_in"), [sem(f"a_weights_in{i}") for i in range(2)], sem("a_xT_in"), sem("a_x_in")
        s_stage, s_fill = sem("a_stage_in"), sem("a_filled")
        s_whi, s_wlo = sem("a_w_hi"), sem("a_w_lo")
        s_xhi, s_xlo = sem("a_x_hi"), sem("a_x_lo")
        s_q, s_kv = sem("a_q"), sem("a_kv")
        s_rq, s_rk, s_rot, s_v1 = sem("a_q_turned"), sem("a_k_turned"), sem("a_rotated"), sem("a_v1")
        s_hi3, s_q3lo, s_k3a, s_k3lo = sem("a_stack_hi"), sem("a_q3_lo"), sem("a_k3_first"), sem("a_k3")
        s_t3, s_q3T, s_k3T = sem("a_stacks_transposed"), sem("a_q3T"), sem("a_k3T")
        s_s, s_mx, s_sub, s_p = sem("a_scores"), sem("a_max"), sem("a_minus_max"), sem("a_probs")
        s_pt, s_ptc, s_pv = sem("a_probs_transposed"), sem("a_prT"), sem("a_pv")
        s_rs, s_on, s_onT = sem("a_recip_sums"), sem("a_on"), sem("a_on_transposed")
        s_onhi, s_onlo, s_wout = sem("a_onT_hi"), sem("a_onT_lo"), sem("a_wout")
        s_y, s_bn, s_mv, s_r, s_x1, s_acc = (sem("a_" + n) for n in ("y", "bn", "mean_var", "inverse_roots", "x1", "acc"))
        s_xn, s_xnT, s_xnhi, s_xnlo = sem("a_xn"), sem("a_xn_transposed"), sem("a_xnT_hi"), sem("a_xnT_lo")
        c_pool = sem("a_pool_chain")

        block = ctx.enter_context(nc.Block())

        def tile(t, j, back):
            b = t - 1 if j >= back else t - 2
            return b, (j - back) % G1, b * G1 + (j - back) % G1

        @block.sync
        def _(sp):
            for c in range(KC):
                if c >= 2:
                    sp.wait_ge(s_wlo, c - 1)
                sp.dma_start(w_raw[c % 2][:], a["w1"][c]).then_inc(s_w[c % 2], 16)
                if c == 0:
                    sp.dma_start(xT_raw[:], a["xT"][0]).then_inc(s_x, 16)
                if c == 1:
                    sp.dma_start(ident[:], a["ident"]).then_inc(s_const, 16)
                    sp.dma_start(rope[:], a["rope"]).then_inc(s_const, 16)
                    sp.dma_start(causal[:], a["causal"]).then_inc(s_const, 16)
                    sp.dma_start(lnw[:], a["lnw"].partition_broadcast(P)).then_inc(s_const, 16)
            with sp.Fori(1, B) as b:
                sp.wait_ge(s_xlo, b)
                sp.dma_start(xT_raw[:], a["xT"][bass.ds(b, 1)].rearrange("b p c t -> p (b c) t")).then_inc(s_x, 16)

        @block.gpsimd
        def _(pool):
            nc.gpsimd.memset(minus_half[:], -0.5)
            nc.gpsimd.memset(eps[:], LN_EPS)
            nc.gpsimd.memset(v1[:], 1.0)
            nc.gpsimd.memset(q3[:], 0.0)
            nc.gpsimd.memset(k3[:], 0.0)
            nc.gpsimd.memset(f32(k3T[:]), 0.0).then_inc(s_fill, 1)
            pool.wait_ge(s_fill, 1)
            nc.gpsimd.dma_start(acc[:], a["x"]).then_inc(s_res, 16)
            nc.gpsimd.dma_start(stage[:], a["cT"]).then_inc(s_stage, 16)

            def step(t, par):
                for j in range(G1):
                    if live(t - 1):
                        n = (t - 1) * G1 + j
                        pool.wait_ge(s_mx, n + 1)
                        nc.gpsimd.tensor_tensor(sm[:, j % 2], sm[:, j % 2],
                                                mx[:, j % 2].rearrange("p (r one) -> p r one", one=1)
                                                .broadcast_to([P, R1, T]), ALU.subtract).then_inc(s_sub, 1)
                    if j == 0 and live(t):
                        pool.wait_ge(s_xhi, t + 1)
                        nc.gpsimd.tensor_tensor(xT[1][:], xT_raw[:], f32(xT[0][:]), ALU.subtract).then_inc(s_xlo, 1)
                    if j == 3 and live(t):
                        pool.wait_ge(s_rk, t + 1)
                        at_least(pool, s_k3lo, t)
                        nc.gpsimd.tensor_tensor(rot[:], rot_a[:], rot_b[:], ALU.add).then_inc(s_rot, 1)
                    if j == 4 and live(t - 2):
                        link = Chain(pool, c_pool, 4 * (t - 2))
                        pool.wait_ge(s_mv, t - 1)
                        link.link(nc.gpsimd.tensor_tensor(cols[:, 0:1], mv[:, 1:2], eps[:], ALU.add))
                        link.link(nc.gpsimd.tensor_tensor(cols[:, 0:1], cols[:, 0:1], minus_half[:], ALU.pow))
                        link.link(nc.gpsimd.tensor_tensor(cols[:, 1:2], cols[:, 0:1], cols[:, 0:1], ALU.mult))
                        nc.gpsimd.tensor_tensor(cols[:, 1:2], cols[:, 1:2], mv[:, 1:2], ALU.mult).then_inc(c_pool, 1)
                        assert link.n == 3
                        pool.wait_ge(c_pool, 4 * (t - 2) + 4)
                        nc.gpsimd.tensor_tensor(cols[:, 2:3], cols[:, 1:2], eps[:], ALU.add)\
                            .then_inc(s_r, 1)
                        pool.wait_ge(s_r, 2 * (t - 2) + 1)
                        nc.gpsimd.tensor_tensor(cols[:, 3:4], cols[:, 2:3], minus_half[:], ALU.pow).then_inc(s_r, 1)
                    if j == 5 and live(t):
                        pool.wait_ge(s_hi3, t + 1)
                        nc.gpsimd.tensor_tensor(q3[:, :, 2 * DH1:3 * DH1],
                                                rot[:, 0:D].rearrange("p (h d) -> p h d", d=DH1),
                                                q3[:, :, 0:DH1], ALU.subtract).then_inc(s_q3lo, 1)
                    if j == 5 and live(t - 2):
                        pool.wait_ge(s_x1, t - 1)
                        nc.gpsimd.tensor_tensor(acc[:, bass.ds(t - 2, 1), :].rearrange("p b d -> p (b d)"), x1[:],
                                                x1[:], ALU.add).then_inc(s_acc, 1)
            steps(pool, step)

        @block.scalar
        def _(act):
            for c in range(KC):
                act.wait_ge(s_w[c % 2], 16 * (c // 2) + 16)
                nc.scalar.copy(w[0][:, c], w_raw[c % 2][:]).then_inc(s_whi, 1)
            act.wait_ge(s_fill, 1)

            def step(t, par):
                for j in range(G1):
                    b, i, n = tile(t, j, 1)
                    if live(b):
                        act.wait_ge(s_sub, n + 1)
                        at_least(act, s_pt, n - 1)
                        nc.scalar.activation(pr[:, i % 2], sm[:, i % 2], ACT.Exp).then_inc(s_p, 1)
                    b, i, n = tile(t, j, 2)
                    if live(b):
                        act.wait_ge(s_pt, n + 1)
                        at_least(act, s_pv, n - 1)
                        nc.scalar.copy(prT[:, i % 2], PT[:].rearrange("p (r t) -> p r t", r=R1)).then_inc(s_ptc, 1)
                    if j == 0 and live(t):
                        act.wait_ge(s_x, 16 * t + 16)
                        at_least(act, s_kv, t)
                        nc.scalar.copy(xT[0][:], xT_raw[:]).then_inc(s_xhi, 1)
                    if j == 2 and live(t - 2):
                        act.wait_ge(s_onT, t - 1)
                        nc.scalar.copy(onT[0][:], TA[:].rearrange("p (c t) -> p c t", c=KC)).then_inc(s_onhi, 1)
                    if j == 4 and live(t):
                        act.wait_ge(s_rot, t + 1)
                        nc.scalar.copy(q3[:, :, 0:2 * DH1].bitcast(F32R).rearrange("p h (two d) -> p h two d", two=2),
                                       rot[:, 0:D].rearrange("p (h one d) -> p h one d", one=1, d=DH1)
                                       .broadcast_to([P, H1, 2, DH1]))
                        nc.scalar.copy(k3[:, :, 0, 0:DH1].bitcast(F32R),
                                       rot[:, D:D + KV1].rearrange("p (g d) -> p g d", d=DH1)).then_inc(s_hi3, 1)
                    if j == 6 and live(t - 2):
                        act.wait_ge(s_xnT, t - 1)
                        nc.scalar.copy(xnT[0][:, :, bass.ds((t - 2) * T, T)],
                                       KVB[:].rearrange("p (c t) -> p c t", c=KC)).then_inc(s_xnhi, 1)
                    if j >= 6 and live(t):
                        for m in (range(2) if j == 6 else range(2, 6)):
                            act.wait_ge(s_t3, 6 * t + m + 1)
                            src = tb[m % 2][:].rearrange("p (h t) -> p h t", h=4)
                            if m < 4:
                                nc.scalar.copy(q3T[:, par, 4 * m:4 * m + 4, :], src).then_inc(s_q3T, 1)
                                continue
                            g = slice(4 * (m - 4), 4 * (m - 4) + 4)
                            nc.scalar.copy(k3T[0:STK, par, g, 0:T], src[0:STK])
                            nc.scalar.copy(k3T[STK:P, par, g, T:2 * T], src[STK:P]).then_inc(s_k3T, 1)
            steps(act, step)

        @block.vector
        def _(dve):
            for c in range(KC):
                dve.wait_ge(s_whi, c + 1)
                nc.vector.tensor_tensor(w[1][:, c], w_raw[c % 2][:], f32(w[0][:, c]), ALU.subtract).then_inc(s_wlo, 1)
            dve.wait_ge(s_const, 64)
            dve.wait_ge(s_fill, 1)

            def turn(ps, lo, n, tab):
                half, nh = DH1 // 2, n // DH1
                src = ps[:, 0:n].rearrange("p (h d) -> p h d", d=DH1)
                ra = rot_a[:, lo:lo + n].rearrange("p (h d) -> p h d", d=DH1)
                rb = rot_b[:, lo:lo + n].rearrange("p (h d) -> p h d", d=DH1)

                def table(i, x, y):
                    return rope[:, tab + i:tab + i + 1, x:y].broadcast_to([P, nh, y - x])
                nc.vector.tensor_tensor(ra, src, table(0, 0, DH1), ALU.mult)
                nc.vector.tensor_tensor(rb[:, :, 0:half], src[:, :, half:DH1], table(1, 0, half), ALU.mult)
                return nc.vector.tensor_tensor(rb[:, :, half:DH1], src[:, :, 0:half], table(1, half, DH1), ALU.mult)

            def normalise(b, i):
                o = o_bank[i][:, 0:HB * (DH1 + 1)].rearrange("p (h d) -> p h d", d=DH1 + 1)
                hs = slice(i * HB, (i + 1) * HB)
                dve.wait_ge(s_pv, G1 * b + (i + 1) * G1 // 2)
                nc.vector.reciprocal(rs[:, hs], o[:, :, DH1]).then_inc(s_rs, 1)
                dve.wait_ge(s_rs, 2 * b + i + 1)
                nc.vector.tensor_tensor(on[:, hs, :], o[:, :, 0:DH1],
                                        rs[:, hs].rearrange("p (h one) -> p h one", one=1)
                                        .broadcast_to([P, HB, DH1]), ALU.mult).then_inc(s_on, 1)

            def step(t, par):
                for j in range(G1):
                    if live(t - 1):
                        n = (t - 1) * G1 + j
                        dve.wait_ge(s_s, n + 1)
                        at_least(dve, s_p, n - 1)
                        gate(nc, spare[:, j % 2:j % 2 + 1])
                        for r in range(R1):
                            ins = nc.vector.tensor_tensor_reduce(
                                sm[:, j % 2, r], s_bank[j % 2][:, r * T:(r + 1) * T], causal[:], 1.0, MASKED,
                                ALU.add, ALU.max, mx[:, j % 2, r:r + 1])
                        ins.then_inc(s_mx, 1)
                    if j == 1 and live(t - 2):
                        normalise(t - 2, 1)
                    if j == 2 and live(t):
                        dve.wait_ge(s_q, t + 1)
                        turn(QB, 0, D, 0).then_inc(s_rq, 1)
                    if j == 3 and live(t - 2):
                        dve.wait_ge(s_onhi, t - 1)
                        nc.vector.tensor_tensor(onT[1][:], TA[:].rearrange("p (c t) -> p c t", c=KC), f32(onT[0][:]),
                                                ALU.subtract).then_inc(s_onlo, 1)
                    if j == 3 and live(t):
                        dve.wait_ge(s_kv, t + 1)
                        turn(KVB, D, KV1, 2).then_inc(s_rk, 1)
                        nc.vector.tensor_copy(v1[:, par, :, 0:DH1],
                                              KVB[:, KV1:2 * KV1].rearrange("p (g d) -> p g d", d=DH1))\
                            .then_inc(s_v1, 1)
                    if j == 4 and live(t - 2):
                        dve.wait_ge(s_wout, t - 1)
                        at_least(dve, s_res, 16)
                        nc.vector.tensor_tensor(y[:], QB[:], acc[:, bass.ds(t - 2, 1), :].rearrange("p b d -> p (b d)"),
                                                ALU.add).then_inc(s_y, 1)
                        dve.wait_ge(s_y, t - 1)
                        nc.vector.bn_stats(st[:], y[:]).then_inc(s_bn, 1)
                        dve.wait_ge(s_bn, t - 1)
                        gate(nc, spare[:, 2:3])
                        nc.vector.bn_aggr(mv[:], st[:]).then_inc(s_mv, 1)
                    if j == 5 and live(t):
                        dve.wait_ge(s_hi3, t + 1)
                        nc.vector.tensor_copy(k3[:, :, 0, 2 * DH1:3 * DH1], k3[:, :, 0, 0:DH1])
                        nc.vector.tensor_tensor(k3[:, :, 0, DH1:2 * DH1],
                                                rot[:, D:D + KV1].rearrange("p (g d) -> p g d", d=DH1),
                                                k3[:, :, 0, 0:DH1], ALU.subtract).then_inc(s_k3a, 1)
                        dve.wait_ge(s_k3a, t + 1)
                        nc.vector.tensor_copy(k3[:, :, 1, 0:3 * DH1], k3[:, :, 0, 0:3 * DH1]).then_inc(s_k3lo, 1)
                    if j == 5 and live(t - 2):
                        dve.wait_ge(s_r, 2 * (t - 1))
                        nc.vector.tensor_scalar(x1[:], y[:], mv[:, 0:1], cols[:, 0:1], ALU.subtract, ALU.mult)\
                            .then_inc(s_x1, 1)
                        dve.wait_ge(s_x1, t - 1)
                        nc.vector.scalar_tensor_tensor(out=xn[:], in0=x1[:], scalar=cols[:, 3:4], in1=lnw[:],
                                                       op0=ALU.mult, op1=ALU.mult).then_inc(s_xn, 1)
                    if j == 6 and live(t - 1):
                        normalise(t - 1, 0)
                    if j == 7 and live(t - 2):
                        dve.wait_ge(s_xnhi, t - 1)
                        nc.vector.tensor_tensor(xnT[1][:, :, bass.ds((t - 2) * T, T)],
                                                KVB[:].rearrange("p (c t) -> p c t", c=KC),
                                                f32(xnT[0][:, :, bass.ds((t - 2) * T, T)]), ALU.subtract)\
                            .then_inc(s_xnlo, 1)
            steps(dve, step)

        @block.tensor
        def _(pe):
            pe.wait_ge(s_const, 64)
            pe.wait_ge(s_wlo, KC)

            def four(bank, blocks):
                for k, blk in enumerate(blocks):
                    ins = nc.tensor.transpose(bank[:, k * T:(k + 1) * T], blk, ident[:])
                return ins

            def x_times(bank, lo, n):
                return product(nc, bank[:, 0:n], [[(xT[p][:, c, :], w[q][:, c, lo:lo + n]) for c in range(KC)]
                                                  for p, q in PARTS])

            def stacks(t, m):
                if m == 0:
                    pe.wait_ge(s_q3lo, t + 1)
                    pe.wait_ge(s_k3lo, t + 1)
                    if live(t - 2):
                        pe.wait_ge(s_onlo, t - 1)
                if m == 1 and live(t - 2):
                    pe.wait_ge(s_y, t - 1)
                if m >= 2:
                    pe.wait_ge(s_q3T, 4 * t + m - 1)
                four(tb[m % 2], [q3[:, 8 * m + 2 * k:8 * m + 2 * k + 2, :].rearrange("p h s -> p (h s)") if m < 4 else
                                 k3[:, 4 * (m - 4) + k].rearrange("p two s -> p (two s)") for k in range(4)])\
                    .then_inc(s_t3, 1)

            def step(t, par):
                for j in range(G1):
                    if live(t - 1):
                        n = (t - 1) * G1 + j
                        if j == 0:
                            pe.wait_ge(s_q3T, 4 * t)
                            pe.wait_ge(s_k3T, 2 * t)
                        at_least(pe, s_mx, n - 1)
                        for k in range(2):
                            ins = nc.tensor.matmul(s_bank[j % 2][:, 2 * k * T:2 * (k + 1) * T],
                                                   q3T[:, 1 - par, 2 * j + k, :], k3T[:, 1 - par, j, :],
                                                   start=True, stop=True)
                        ins.then_inc(s_s, 1)
                    b, i, n = tile(t, j, 2)
                    if live(b):
                        pe.wait_ge(s_p, n + 1)
                        four(PT, [pr[:, i % 2, r] for r in range(R1)]).then_inc(s_pt, 1)
                    if j == 1 and live(t):
                        pe.wait_ge(s_xlo, t + 1)
                        x_times(QB, 0, D).then_inc(s_q, 1)
                    if j == 2 and live(t):
                        x_times(KVB, D, 2 * KV1).then_inc(s_kv, 1)
                    if j == 2 and live(t - 2):
                        pe.wait_ge(s_on, 2 * (t - 1))
                        four(TA, [on[:, 8 * c:8 * c + 8, :].rearrange("p h d -> p (h d)") for c in range(KC)])\
                            .then_inc(s_onT, 1)
                    if j == 3 and live(t - 2):
                        pe.wait_ge(s_onlo, t - 1)
                        if live(t):
                            pe.wait_ge(s_rq, t + 1)
                        product(nc, QB[:], [[(onT[p][:, c, :], w[q][:, c, NW - D:]) for c in range(KC)]
                                            for p, q in PARTS]).then_inc(s_wout, 1)
                    if j == 6 and live(t - 2):
                        pe.wait_ge(s_xn, t - 1)
                        if live(t):
                            pe.wait_ge(s_v1, t + 1)
                        four(KVB, [xn[:, c * P:(c + 1) * P] for c in range(KC)]).then_inc(s_xnT, 1)
                    if j == 6 and live(t):
                        for m in range(2):
                            stacks(t, m)
                    if j == 7 and live(t):
                        for m in range(2, 6):
                            stacks(t, m)
                    if live(b):
                        pe.wait_ge(s_ptc, n + 1)
                        if i in (0, G1 // 2):
                            at_least(pe, s_on, 2 * b - 1 + 2 * i // G1)
                            pe.wait_ge(s_v1, b + 1)
                        for r in range(R1):
                            h = R1 * i + r
                            col = (h % HB) * (DH1 + 1)
                            ins = nc.tensor.matmul(o_bank[h // HB][:, col:col + DH1 + 1], prT[:, i % 2, r],
                                                   v1[:, par if j < 2 else 1 - par, i, :],
                                                   start=True, stop=True)
                        ins.then_inc(s_pv, 1)
            steps(pe, step)
    return s_stage


def product(nc, out, parts, start=True):
    pairs = [p for part in parts for p in part]
    for i, (lhs, rhs) in enumerate(pairs):
        ins = nc.tensor.matmul(out, lhs, rhs, start=start and i == 0, stop=i == len(pairs) - 1)
    return ins


def cross_attention(nc, a, whole, sb, sem, banks, xnT, acc, stage, s_stage, ident, spare):
    with ExitStack() as ctx:
        cT = [sb(ctx, f"cT_{s}", [P, KC, B * T], F32R) for s in ("hi", "lo")]
        mask8 = sb(ctx, "mask8", [P, B, T], U8)
        mask = sb(ctx, "mask", [P, B, T])
        qk_raw = [sb(ctx, f"qk_raw{i}", [P, 2, KC, P]) for i in range(HG)]
        v_raw = sb(ctx, "v_raw", [P, KC, HG * DH2])
        o_raw = sb(ctx, "o_raw", [P, HG, D])
        wqk = [[sb(ctx, f"wqk{i}_{s}", [P, 2, KC, P], F32R) for s in ("hi", "lo")] for i in range(HG)]
        wv = [sb(ctx, f"wv_{s}", [P, KC, HG * DH2], F32R) for s in ("hi", "lo")]
        wo = [sb(ctx, f"wo_{s}", [P, HG, D], F32R) for s in ("hi", "lo")]
        bias = sb(ctx, "bias", [P, HG, T])
        bm = sb(ctx, "bm", [P, 2, HALF, T])
        qT = sb(ctx, "qT", [P, 2, HALF * T])
        kT = sb(ctx, "kT", [P, 2, HALF * T])
        v = sb(ctx, "v", [P, B, HG * DH2])
        sm = sb(ctx, "sm", [P, 2, HALF, T])
        pr = sb(ctx, "pr", [P, 2, HALF, T])
        prT = sb(ctx, "prT", [P, HALF, T])
        mx = sb(ctx, "mx", [P, 2, HALF])
        nmx = sb(ctx, "nmx", [P, 2, HALF])
        sums = sb(ctx, "sums", [P, 2, HALF])
        rsum = sb(ctx, "rsum", [P, 2, HALF])
        at = [sb(ctx, f"at_{s}", [P, 2, HG, HALF * T], F32R) for s in ("hi", "lo")]

        S = banks[0:2]
        PQ, PK, PT, PO = banks[2:6]
        PX = banks[6:8]

        s_mask_in, s_experts_in = sem("b_mask_in"), sem("b_experts_in")
        s_chi, s_clo = sem("b_ctx_hi"), sem("b_ctx_lo")
        s_mask = sem("b_mask")
        s_qk_in = [sem(f"b_qk{i}_in") for i in range(HG)]
        s_v_in, s_o_in, s_bias_in = sem("b_v_in"), sem("b_o_in"), sem("b_bias_in")
        s_wqk_h = [sem(f"b_wqk{i}_hi") for i in range(HG)]
        s_wqk = [sem(f"b_wqk{i}") for i in range(HG)]
        s_wv_h, s_wv = sem("b_wv_hi"), sem("b_wv")
        s_wo_h, s_wo = sem("b_wo_hi"), sem("b_wo")
        s_bm = sem("b_bias_mask")
        s_q, s_k, s_qT, s_kT = sem("b_q"), sem("b_k"), sem("b_qT"), sem("b_kT")
        s_v, s_vc = sem("b_v"), sem("b_v_copied")
        s_s, s_nm, s_e, s_p = sem("b_scores"), sem("b_negmax"), sem("b_exp"), sem("b_probs")
        s_t, s_prT, s_pv = sem("b_probs_transposed"), sem("b_prT"), sem("b_pv")
        s_ah, s_al = sem("b_at_hi"), sem("b_at_lo")
        s_out, s_acc = sem("b_out"), sem("b_acc")
        c_dve = sem("b_dve_chain")
        DVE_CHAIN = 3

        block = ctx.enter_context(nc.Block())

        def one(ap, g):
            return ap[bass.ds(g, 1)]

        def groups(eng, step):
            step(0, True, False)
            with eng.Fori(1, NG - 1) as g:
                step(g, False, False)
            step(NG - 1, False, True)

        def old_out(g, s, first):
            if first:
                return None
            return (B * (g - 1), B * (g - 1) + HALF, B * (g - 1) + HALF, B * g)[s]

        @block.sync
        def _(sp):
            def load_qk(i, g):
                sp.dma_start(qk_raw[i][:], one(a["wqk"], g)[:, :, i].rearrange("g p q c j -> p (g q) c j"))\
                    .then_inc(s_qk_in[i], 16)

            def load_v(g):
                sp.dma_start(v_raw[:], one(a["wv"], g).rearrange("g p c j -> p (g c) j")).then_inc(s_v_in, 16)

            def load_o(g):
                sp.dma_start(o_raw[:], one(a["wo"], g).rearrange("g p i n -> p (g i) n")).then_inc(s_o_in, 16)

            def load_bias(g):
                sp.dma_start(bias[:], one(a["bias"], g).rearrange("g p i k -> p (g i) k")).then_inc(s_bias_in, 16)

            load_qk(0, 0)
            load_v(0)
            load_qk(1, 0)
            sp.dma_start(mask8[:], a["mask"]).then_inc(s_mask_in, 16)
            load_bias(0)
            load_o(0)
            sp.wait_ge(s_clo, KC)
            at = 0
            for name in EXPERT_INPUTS:
                n = a[name].shape[1]
                sp.dma_start(stage[:, at:at + n], a[name]).then_inc(s_experts_in, 16)
                at += n
            with sp.Fori(0, NG - 1) as g:
                sp.wait_ge(s_wv, g + 1)
                load_v(g + 1)
                sp.wait_ge(s_wqk[0], g + 1)
                load_qk(0, g + 1)
                sp.wait_ge(s_wqk[1], g + 1)
                load_qk(1, g + 1)
                sp.wait_ge(s_wo, g + 1)
                load_o(g + 1)
                sp.wait_ge(s_bm, TILES * g + TILES)
                load_bias(g + 1)

        @block.gpsimd
        def _(pool):
            def bias_mask(g, s, first):
                n = TILES * g + s
                if s == 0:
                    pool.wait_ge(s_bias_in, 16 * g + 16)
                if not first or s >= 2:
                    pool.wait_ge(s_nm, n - 1)
                nc.gpsimd.tensor_tensor(bm[:, s % 2], mask[:, HALF * (s // HG):HALF * (s // HG + 1), :],
                                        bias[:, s % HG:s % HG + 1, :].broadcast_to([P, HALF, T]), ALU.add)\
                    .then_inc(s_bm, 1)

            pool.wait_ge(s_mask, 1)
            for s in range(TILES):
                bias_mask(0, s, True)
            with pool.Fori(1, NG) as g:
                for s in range(TILES):
                    bias_mask(g, s, False)

        @block.scalar
        def _(act):
            def hi_qk(i, g, first=False):
                act.wait_ge(s_qk_in[i], 16 * g + 16)
                if not first:
                    act.wait_ge(s_k, TILES * g - 1 + i)
                nc.scalar.copy(wqk[i][0][:], qk_raw[i][:]).then_inc(s_wqk_h[i], 1)

            def hi_v(g, first=False):
                act.wait_ge(s_v_in, 16 * g + 16)
                if not first:
                    act.wait_ge(s_v, B * g)
                nc.scalar.copy(wv[0][:], v_raw[:]).then_inc(s_wv_h, 1)

            def hi_o(g, first):
                act.wait_ge(s_o_in, 16 * g + 16)
                if not first:
                    act.wait_ge(s_out, B * g)
                nc.scalar.copy(wo[0][:], o_raw[:]).then_inc(s_wo_h, 1)

            def copy_qk(n, m):
                act.wait_ge(s_q, n + 1)
                nc.scalar.copy(qT[:, m % 2], PQ[:]).then_inc(s_qT, 1)
                act.wait_ge(s_k, n + 1)
                nc.scalar.copy(kT[:, m % 2], PK[:]).then_inc(s_kT, 1)

            def copy_v(c, b, used):
                act.wait_ge(s_v, c + 1)
                if used is not None:
                    act.wait_ge(s_pv, used)
                nc.scalar.copy(v[:, b, :], PX[b % 2][:, 0:HG * DH2]).then_inc(s_vc, 1)

            def exps(n, s, first):
                act.wait_ge(s_nm, n + 1)
                if not first or s >= 2:
                    act.wait_ge(s_t, n - 1)
                for k in range(HALF):
                    e = nc.scalar.activation(pr[:, s % 2, k], sm[:, s % 2, k], ACT.Exp,
                                             bias=nmx[:, s % 2, k:k + 1], accum_out=sums[:, s % 2, k:k + 1])
                e.then_inc(s_e, 1)

            def copy_prT(n, first):
                act.wait_ge(s_t, n + 1)
                if not first:
                    act.wait_ge(s_pv, n)
                nc.scalar.copy(prT[:], PT[:].rearrange("p (b t) -> p b t", b=HALF)).then_inc(s_prT, 1)

            def at_hi(n, s, used):
                act.wait_ge(s_pv, n + 1)
                if used is not None:
                    act.wait_ge(s_out, used)
                nc.scalar.copy(at[0][:, s // HG, s % HG], PO[:]).then_inc(s_ah, 1)

            def step(g, first, last):
                for s in range(TILES):
                    n = TILES * g + s
                    if s == 2:
                        if not last:
                            hi_v(g + 1)
                        hi_o(g, first)
                        if not last:
                            hi_qk(0, g + 1)
                    if s == 3 and not last:
                        hi_qk(1, g + 1)
                    exps(n, s, first)
                    if not (last and s == TILES - 1):
                        copy_qk(n + 1, s + 1)
                    prev = not (first and s == 0)
                    if prev:
                        copy_prT(n - 1, first and s == 1)
                    b = (HALF + 2 * s) % B
                    has_v = not (last and s >= 2)
                    used = (None if first else TILES * g) if s < 2 else TILES * g + 2
                    if has_v:
                        copy_v(2 * n + HALF, b, used)
                    if prev:
                        at_hi(n - 1, (s - 1) % TILES, old_out(g, s, first))
                    if has_v:
                        copy_v(2 * n + HALF + 1, b + 1, used)
                if last:
                    n = TILES * NG
                    copy_prT(n - 1, False)
                    at_hi(n - 1, TILES - 1, B * (NG - 1))

            hi_qk(0, 0, True)
            act.wait_ge(s_stage, 16)
            for c in range(KC):
                nc.scalar.copy(cT[0][:, c, :], stage[:, c * B * T:(c + 1) * B * T]).then_inc(s_chi, 1)
            hi_v(0, True)
            hi_qk(1, 0, True)
            copy_qk(0, 0)
            for b in range(HALF):
                copy_v(b, b, None)
            groups(act, step)

        @block.vector
        def _(dve):
            def lo(parts, raw, s_h, s_done, count):
                dve.wait_ge(s_h, count)
                nc.vector.tensor_tensor(parts[1][:], raw[:], f32(parts[0][:]), ALU.subtract).then_inc(s_done, 1)

            def masked_scores(n, s, first, link):
                dve.wait_ge(s_s, n + 1)
                dve.wait_ge(s_bm, n + 1)
                if not first or s >= 2:
                    dve.wait_ge(s_e, n - 1)
                gate(nc, spare[:, s % 2:s % 2 + 1])
                for k in range(HALF):
                    ins = nc.vector.tensor_tensor_reduce(sm[:, s % 2, k], S[s % 2][:, k * T:(k + 1) * T],
                                                         bm[:, s % 2, k], 1.0, FLOOR, ALU.add, ALU.max,
                                                         mx[:, s % 2, k:k + 1])
                link.link(ins)
                nc.vector.tensor_scalar(nmx[:, s % 2], mx[:, s % 2], -1.0, None, ALU.mult).then_inc(s_nm, 1)

            def normalise(n, s, link):
                dve.wait_ge(s_e, n + 1)
                link.link(nc.vector.tensor_scalar(rsum[:, s % 2], sums[:, s % 2], 0.5, None, ALU.max))
                link.link(nc.vector.reciprocal(rsum[:, s % 2], rsum[:, s % 2]))
                nc.vector.tensor_tensor(pr[:, s % 2], pr[:, s % 2],
                                        rsum[:, s % 2].rearrange("p (b one) -> p b one", one=1)
                                        .broadcast_to([P, HALF, T]), ALU.mult).then_inc(s_p, 1)

            def at_lo(n, s):
                dve.wait_ge(s_ah, n + 1)
                nc.vector.tensor_tensor(at[1][:, s // HG, s % HG], PO[:], f32(at[0][:, s // HG, s % HG]),
                                        ALU.subtract).then_inc(s_al, 1)

            def accumulate(n, j, b):
                dve.wait_ge(s_out, 2 * n - HALF + j + 1)
                dve.wait_ge(s_acc, 2 * n - HALF)
                nc.vector.tensor_tensor(acc[:, b], acc[:, b], PX[b % 2][:], ALU.add).then_inc(s_acc, 1)

            def step(g, first, last):
                for s in range(TILES):
                    n = TILES * g + s
                    link = Chain(dve, c_dve, DVE_CHAIN * n)
                    if s == 2 and not last:
                        lo(wv, v_raw, s_wv_h, s_wv, g + 2)
                    if s == 2:
                        lo(wo, o_raw, s_wo_h, s_wo, g + 1)
                    masked_scores(n, s, first, link)
                    if s == 2 and not last:
                        lo(wqk[0], qk_raw[0], s_wqk_h[0], s_wqk[0], g + 2)
                    if s == 3 and not last:
                        lo(wqk[1], qk_raw[1], s_wqk_h[1], s_wqk[1], g + 2)
                    normalise(n, s, link)
                    assert link.n == DVE_CHAIN
                    if not (first and s == 0):
                        at_lo(n - 1, (s - 1) % TILES)
                    if not (first and s < 2):
                        for j in range(2):
                            accumulate(n, j, (HALF + 2 * s + j) % B)
                if last:
                    n = TILES * NG
                    at_lo(n - 1, TILES - 1)
                    for j in range(HALF):
                        accumulate(n, j, HALF + j)

            dve.wait_ge(s_mask_in, 16)
            nc.vector.tensor_scalar(mask[:], mask8[:], -1.0, -MASKED, ALU.add, ALU.mult).then_inc(s_mask, 1)
            lo(wqk[0], qk_raw[0], s_wqk_h[0], s_wqk[0], 1)
            for c in range(KC):
                dve.wait_ge(s_chi, c + 1)
                nc.vector.tensor_tensor(cT[1][:, c, :], stage[:, c * B * T:(c + 1) * B * T], f32(cT[0][:, c, :]),
                                        ALU.subtract).then_inc(s_clo, 1)
            lo(wv, v_raw, s_wv_h, s_wv, 1)
            lo(wqk[1], qk_raw[1], s_wqk_h[1], s_wqk[1], 1)
            groups(dve, step)

        @block.tensor
        def _(pe):
            def project_qk(g, m, start=False):
                i, half = m % HG, m // HG
                tok = slice(half * HALF * T, (half + 1) * HALF * T)
                pe.wait_ge(s_wqk[i], g + 1)
                product(nc, PQ[:], [[(wqk[i][p][:, 0, c], xnT[q][:, c, tok]) for c in range(KC)] for p, q in PARTS])\
                    .then_inc(s_q, 1)
                if start:
                    pe.wait_ge(s_clo, KC)
                product(nc, PK[:], [[(wqk[i][p][:, 1, c], cT[q][:, c, tok]) for c in range(KC)] for p, q in PARTS])\
                    .then_inc(s_k, 1)

            def project_v(b):
                product(nc, PX[b % 2][:, 0:HG * DH2],
                        [[(cT[p][:, c, b * T:(b + 1) * T], wv[q][:, c, :]) for c in range(KC)] for p, q in PARTS])\
                    .then_inc(s_v, 1)

            def scores(n, s, first):
                pe.wait_ge(s_kT, n + 1)
                if not first or s >= 2:
                    pe.wait_ge(s_nm, n - 1)
                for k in range(HALF):
                    tok = slice(k * T, (k + 1) * T)
                    ins = nc.tensor.matmul(S[s % 2][:, tok], qT[:, s % 2, tok], kT[:, s % 2, tok],
                                           start=True, stop=True)
                ins.then_inc(s_s, 1)

            def transposes(n, s):
                pe.wait_ge(s_p, n + 1)
                for k in range(HALF):
                    ins = nc.tensor.transpose(PT[:, k * T:(k + 1) * T], pr[:, s % 2, k], ident[:])
                ins.then_inc(s_t, 1)

            def pv(n, s, v_ready, first):
                pe.wait_ge(s_prT, n + 1)
                pe.wait_ge(s_vc, v_ready)
                if not first:
                    pe.wait_ge(s_al, n)
                half, i = s // HG, s % HG
                for k in range(HALF):
                    ins = nc.tensor.matmul(PO[:, k * T:(k + 1) * T], v[:, half * HALF + k, i * DH2:(i + 1) * DH2],
                                           prT[:, k], start=True, stop=True)
                ins.then_inc(s_pv, 1)

            def output(b, half):
                tok = slice((b - half * HALF) * T, (b - half * HALF + 1) * T)
                product(nc, PX[b % 2][:], [[(at[p][:, half, i, tok], wo[q][:, i, :]) for i in range(HG)]
                                           for p, q in PARTS]).then_inc(s_out, 1)

            def step(g, first, last):
                for s in range(TILES):
                    n = TILES * g + s
                    prev, sp = not (first and s == 0), (s - 1) % TILES
                    has_v = not (last and s >= 2)
                    had_out = not (first and s < 3)
                    scores(n, s, first)
                    if not (last and s == TILES - 1):
                        project_qk(g if s < TILES - 1 else g + 1, (s + 1) % TILES)
                    if prev:
                        transposes(n - 1, sp)
                    for j in range(2):
                        if has_v:
                            b = (HALF + 2 * s + j) % B
                            pe.wait_ge(s_wv, g + 1 if s < 2 else g + 2)
                            if had_out:
                                pe.wait_ge(s_acc, 2 * n - 5 + j)
                            pe.wait_ge(s_vc, 2 * n + 3 + j)
                            project_v(b)
                        if j == 0 and prev:
                            v_ready = B * g if s == 0 else B * g + HALF * (sp // HG + 1)
                            pv(n - 1, sp, v_ready, first and s == 1)
                    if not (first and s < 2):
                        half = 0 if s >= 2 else 1
                        if s in (0, 2):
                            pe.wait_ge(s_al, n)
                        if s == 2:
                            pe.wait_ge(s_wo, g + 1)
                        for j in range(2):
                            if has_v:
                                pe.wait_ge(s_vc, 2 * n + HALF + 1 + j)
                            else:
                                pe.wait_ge(s_acc, 2 * n - 5 + j)
                            output((HALF + 2 * s + j) % B, half)
                if last:
                    n = TILES * NG
                    transposes(n - 1, TILES - 1)
                    pv(n - 1, TILES - 1, B * NG, False)
                    pe.wait_ge(s_al, n)
                    for j in range(HALF):
                        pe.wait_ge(s_acc, 2 * n - 5 + j)
                        output(HALF + j, 1)

            project_qk(0, 0, True)
            pe.wait_ge(s_wv, 1)
            for b in range(HALF):
                if b >= 2:
                    pe.wait_ge(s_vc, b - 1)
                project_v(b)
            groups(pe, step)
    return s_experts_in


EXPERT_INPUTS = ("wbase", "war", "wB", "b_base", "router_b", "prior", "iota")


def experts(nc, a, whole, sb, sem, banks, acc, stage, s_in, ident, spare, out_d):
    at, views = 0, {}
    for name in EXPERT_INPUTS:
        n = a[name].shape[1]
        views[name] = stage[:, at:at + n]
        at += n
    NE = E * RK + E
    wb_raw = views["wbase"].rearrange("p (c n) -> p c n", c=KC)
    war = views["war"].rearrange("p (c n) -> p c n", c=KC)
    wB, b_base, router_b, prior, iota = (views[k] for k in EXPERT_INPUTS[2:])
    with ExitStack() as ctx:
        wb = [sb(ctx, f"wb_{s}", [P, KC, D], F32R) for s in ("hi", "lo")]
        minus_half = sb(ctx, "minus_half2", [P, 1])
        eps = sb(ctx, "eps2", [P, 1])
        active = sb(ctx, "active", [P, EA], I32)
        active_f = sb(ctx, "active_f", [P, EA])
        hit = sb(ctx, "hit", [P, E])
        prior_eps = sb(ctx, "prior_eps", [P, E])
        count = sb(ctx, "count", [P, E])
        logit0 = sb(ctx, "logit0", [P, E])
        x2 = sb(ctx, "x2", [P, D])
        x2T_f = sb(ctx, "x2T_f", [P, KC, T])
        x2T = [sb(ctx, f"x2T_{s}", [P, KC, T], F32R) for s in ("hi", "lo")]
        logit = sb(ctx, "logit", [P, E])
        nmax = sb(ctx, "nmax", [P, 1])
        alpha = sb(ctx, "alpha", [P, E])
        asum = sb(ctx, "asum", [P, 1])
        u = sb(ctx, "u", [P, E, RK])
        uT = sb(ctx, "uT", [P, T])
        y = sb(ctx, "y2", [P, 2, D])
        st = [sb(ctx, f"st2_{k}", [P, 6]) for k in "xy"]
        mv = [sb(ctx, f"mv2_{k}", [P, 2]) for k in "xy"]
        rstd = [sb(ctx, f"rstd_{k}", [P, 1]) for k in "xy"]
        XT, AR, UT = banks[0:3]
        BASE = banks[3:5]

        s_act_in = sem("c_active_in")
        s_whi, s_wlo, s_pe, s_lp = sem("c_w_hi"), sem("c_w_lo"), sem("c_prior_eps"), sem("c_log_prior")
        s_half = sem("c_minus_half")
        s_bn, s_mv, s_ve, s_r = ([sem(f"c_{n}_{k}") for k in "xy"] for n in ("bn", "mean_var", "var_eps", "rstd"))
        s_x2, s_xb, s_xt, s_xh, s_xl = (sem("c_" + n) for n in ("x2", "x2_bias", "x2_transposed", "x2T_hi", "x2T_lo"))
        s_ar, s_lg, s_nm, s_e, s_u, s_ut, s_uc, s_mm = (sem("c_" + n) for n in (
            "experts_a", "logits", "negmax", "alpha_exp", "u", "u_transposed", "uT", "sum"))
        s_y, s_o, s_st = sem("c_y"), sem("c_o"), sem("c_stored")
        c_dve, c_pre = sem("c_dve_chain"), sem("c_pre_chain")
        N_IN = 16 * len(EXPERT_INPUTS)
        SUMS = 4

        block = ctx.enter_context(nc.Block())

        @block.sync
        def _(sp):
            sp.dma_start(active[:], a["active"].partition_broadcast(P)).then_inc(s_act_in, 16)
            with sp.Fori(0, B) as b:
                sp.wait_ge(s_o, b + 1)
                sp.dma_start(out_d[bass.ds(b * T, T), :], acc[:, bass.ds(b, 1), :].rearrange("p b d -> p (b d)"))\
                    .then_inc(s_st, 16)
            sp.wait_ge(s_st, 16 * B)

        @block.gpsimd
        def _(pool):
            nc.gpsimd.memset(eps[:], LN_EPS)
            nc.gpsimd.memset(minus_half[:], -0.5).then_inc(s_half, 1)
            pool.wait_ge(s_half, 1)
            pool.wait_ge(s_in, N_IN)

            def step(t, par):
                for k, b in ((1, t - 2), (0, t)):
                    if live(b):
                        pool.wait_ge(s_mv[k], b + 1)
                        nc.gpsimd.tensor_tensor(rstd[k][:], mv[k][:, 1:2], eps[:], ALU.add)\
                            .then_inc(s_ve[k], 1)
                        pool.wait_ge(s_ve[k], b + 1)
                        nc.gpsimd.tensor_tensor(rstd[k][:], rstd[k][:], minus_half[:], ALU.pow).then_inc(s_r[k], 1)
                if live(t):
                    pool.wait_ge(s_x2, t + 1)
                    nc.gpsimd.tensor_tensor(acc[:, bass.ds(t, 1), :].rearrange("p b d -> p (b d)"), x2[:], b_base,
                                            ALU.add).then_inc(s_xb, 1)
            steps(pool, step)

        @block.scalar
        def _(act):
            act.wait_ge(s_in, N_IN)
            nc.scalar.copy(wb[0][:], wb_raw).then_inc(s_whi, 1)
            act.wait_ge(s_pe, 1)
            nc.scalar.activation(logit0[:], prior_eps[:], ACT.Ln).then_inc(s_lp, 1)

            def step(t, par):
                if live(t - 1):
                    act.wait_ge(s_nm, t)
                    nc.scalar.activation(alpha[:], logit[:], ACT.Exp, bias=nmax[:]).then_inc(s_e, 1)
                if live(t):
                    act.wait_ge(s_xt, t + 1)
                    nc.scalar.copy(x2T[0][:], XT[:].rearrange("p (c t) -> p c t", c=KC))
                    nc.scalar.copy(x2T_f[:], XT[:].rearrange("p (c t) -> p c t", c=KC)).then_inc(s_xh, 1)
                if live(t - 1):
                    act.wait_ge(s_ut, t)
                    nc.scalar.copy(uT[:], UT[:, 0:T]).then_inc(s_uc, 1)
            steps(act, step)

        @block.vector
        def _(dve):
            pre = Chain(dve, c_pre, 0)
            dve.wait_ge(s_act_in, 16)
            dve.wait_ge(s_in, N_IN)
            nc.vector.tensor_scalar(prior_eps[:], prior, PRIOR_EPS, None, ALU.add).then_inc(s_pe, 1)
            pre.link(nc.vector.tensor_copy(active_f[:], active[:]))
            pre.link(nc.vector.tensor_scalar(count[:], iota, active_f[:, 0:1], None, ALU.is_equal))
            for k in range(1, EA):
                pre.link(nc.vector.tensor_scalar(hit[:], iota, active_f[:, k:k + 1], None, ALU.is_equal))
                pre.link(nc.vector.tensor_tensor(count[:], count[:], hit[:], ALU.add))
            dve.wait_ge(s_lp, 1)
            pre.link(nc.vector.tensor_tensor(logit0[:], logit0[:], router_b, ALU.add))
            pre.link(nc.vector.tensor_scalar(hit[:], count[:], 0.0, MASKED, ALU.is_equal, ALU.mult))
            pre.link(nc.vector.tensor_tensor(logit0[:], logit0[:], hit[:], ALU.add))
            dve.wait_ge(s_whi, 1)
            nc.vector.tensor_tensor(wb[1][:], wb_raw, f32(wb[0][:]), ALU.subtract).then_inc(s_wlo, 1)

            def stats(k, src, b):
                nc.vector.bn_stats(st[k][:], src).then_inc(s_bn[k], 1)
                dve.wait_ge(s_bn[k], b + 1)
                gate(nc, spare[:, 2 + k:3 + k])
                nc.vector.bn_aggr(mv[k][:], st[k][:]).then_inc(s_mv[k], 1)

            def norm(k, dst, src, b):
                dve.wait_ge(s_r[k], b + 1)
                return nc.vector.tensor_scalar(dst, src, mv[k][:, 0:1], rstd[k][:], ALU.subtract, ALU.mult)

            def row(b):
                return acc[:, bass.ds(b, 1), :].rearrange("p b d -> p (b d)")

            def step(t, par):
                if live(t - 2):
                    dve.wait_ge(s_mm, t - 1)
                    nc.vector.tensor_tensor(y[:, par], BASE[par][:], row(t - 2), ALU.add).then_inc(s_y, 1)
                if live(t):
                    stats(0, row(t), t)
                if live(t - 2):
                    dve.wait_ge(s_y, t - 1)
                    stats(1, y[:, par], t - 2)
                if live(t - 1):
                    dve.wait_ge(s_ar, t)
                    nc.vector.tensor_tensor(logit[:], AR[:, E * RK:NE], logit0[:], ALU.add).then_inc(s_lg, 1)
                    dve.wait_ge(s_lg, t)
                    nc.vector.tensor_reduce(nmax[:], logit[:], AX_X, ALU.max, negate=True).then_inc(s_nm, 1)
                if live(t):
                    at_least(dve, s_xb, t)
                    norm(0, x2[:], row(t), t).then_inc(s_x2, 1)
                if live(t - 1):
                    link = Chain(dve, c_dve, SUMS * (t - 1))
                    dve.wait_ge(s_e, t)
                    link.link(nc.vector.tensor_tensor(alpha[:], alpha[:], count[:], ALU.mult))
                    link.link(nc.vector.reduce_sum(asum[:], alpha[:], AX_X))
                    link.link(nc.vector.reciprocal(asum[:], asum[:]))
                    link.link(nc.vector.tensor_scalar(alpha[:], alpha[:], asum[:], SCALING, ALU.mult, ALU.mult))
                    assert link.n == SUMS
                    nc.vector.tensor_tensor(u[:], AR[:, 0:E * RK].rearrange("p (e r) -> p e r", r=RK),
                                            alpha[:].rearrange("p (e one) -> p e one", one=1)
                                            .broadcast_to([P, E, RK]), ALU.mult).then_inc(s_u, 1)
                if live(t):
                    dve.wait_ge(s_xh, t + 1)
                    nc.vector.tensor_tensor(x2T[1][:], XT[:].rearrange("p (c t) -> p c t", c=KC), f32(x2T[0][:]),
                                            ALU.subtract).then_inc(s_xl, 1)
                if live(t - 2):
                    norm(1, row(t - 2), y[:, par], t - 2).then_inc(s_o, 1)

            steps(dve, step)

        @block.tensor
        def _(pe):
            pe.wait_ge(s_in, N_IN)
            pe.wait_ge(s_wlo, 1)

            def step(t, par):
                if live(t - 1):
                    pe.wait_ge(s_xl, t)
                    at_least(pe, s_u, t - 1)
                    for c in range(KC):
                        ins = nc.tensor.matmul(AR[:, 0:NE], x2T_f[:, c, :], war[:, c, :],
                                               start=c == 0, stop=c == KC - 1)
                    ins.then_inc(s_ar, 1)
                    pairs = [(x2T[p][:, c, :], wb[q][:, c, :]) for p, q in PARTS for c in range(KC)]
                    for i, (lhs, rhs) in enumerate(pairs):
                        nc.tensor.matmul(BASE[1 - par][:], lhs, rhs, start=i == 0, stop=False)
                if live(t):
                    pe.wait_ge(s_x2, t + 1)
                    for c in range(KC):
                        ins = nc.tensor.transpose(XT[:, c * T:(c + 1) * T], x2[:, c * P:(c + 1) * P], ident[:])
                    ins.then_inc(s_xt, 1)
                if live(t - 1):
                    pe.wait_ge(s_u, t)
                    nc.tensor.transpose(UT[:, 0:T], u[:].rearrange("p e r -> p (e r)"), ident[:]).then_inc(s_ut, 1)
                    pe.wait_ge(s_uc, t)
                    nc.tensor.matmul(BASE[1 - par][:], uT[:], wB, start=False, stop=True).then_inc(s_mm, 1)
            steps(pe, step)


def rope_tables():
    f = np.float32
    inv = (1.0 / np.power(f(500000.0), np.arange(0, DH1, 2, dtype=f) / f(DH1))).astype(f)
    wavelen = (f(2.0 * np.pi) / inv).astype(f)
    lo, hi = 1024 / 4.0, 1024 / 1.0
    inv2 = np.where(wavelen > hi, inv / f(32.0), inv).astype(f)
    smooth = ((f(1024) / wavelen - f(1.0)) / f(3.0)).astype(f)
    smoothed = ((f(1.0) - smooth) * inv2 / f(32.0) + smooth * inv2).astype(f)
    medium = ~(wavelen < hi) & ~(wavelen > lo)
    inv3 = np.where(medium, smoothed, inv2).astype(f)
    freqs = (np.arange(T, dtype=f)[:, None] * inv3[None, :]).astype(f)
    emb = np.concatenate([freqs, freqs], axis=-1)
    cos, sin = np.cos(emb).astype(f), np.sin(emb).astype(f)
    sin = np.concatenate([-sin[:, :DH1 // 2], sin[:, DH1 // 2:]], axis=-1)
    s = f(DH1 ** -0.5)
    return np.ascontiguousarray(np.stack([cos * s, sin * s, cos, sin], axis=1))


def kernel(x, ctx_4096, mask_BxSxS2_bk0, L0_attn_Wq, L0_attn_Wk, L0_attn_Wv, L0_attn_Wo, L0_xattn_position_bias,
           L0_xattn_ln_weight, L0_xattn_w_q, L0_xattn_w_k, L0_xattn_w_v, L0_xattn_w_out, L0_ffn_W_base,
           L0_ffn_b_base, L0_ffn_lora_A, L0_ffn_lora_B, L0_ffn_router_W, L0_ffn_router_b, L0_ffn_domain_prior,
           L0_ffn_active):
    import concourse.bacc as bacc
    from concourse.bass_utils import run_bass_kernel_spmd

    def arr(v):
        return np.asarray(v)

    def rows(v):
        return np.broadcast_to(v, (P, v.shape[0]))

    def chunks(wt):
        return wt.reshape(KC, P, -1).transpose(1, 0, 2)

    def tokens(v):
        return v.reshape(B, T, KC, P).transpose(0, 3, 2, 1)

    def heads(wm):
        return wm.T.reshape(KC, P, NG, HG, DH2).transpose(2, 1, 0, 3, 4)

    xa, wo2 = arr(x), arr(L0_xattn_w_out)
    wqk = np.stack([heads(arr(L0_xattn_w_q)), heads(arr(L0_xattn_w_k))], axis=0)
    tri = np.tril(np.ones((T, T), dtype=bool))
    arrays = {
        "xT": tokens(xa),
        "x": xa.transpose(1, 0, 2),
        "cT": tokens(arr(ctx_4096)).transpose(1, 2, 0, 3).reshape(P, KC * B * T),
        "w1": np.concatenate([arr(L0_attn_Wq).T, arr(L0_attn_Wk).T, arr(L0_attn_Wv).T, arr(L0_attn_Wo).T], axis=1)
        .reshape(KC, P, -1),
        "wqk": wqk.transpose(1, 2, 4, 0, 3, 5),
        "wv": heads(arr(L0_xattn_w_v)).reshape(NG, P, KC, HG * DH2),
        "wo": wo2.T.reshape(NG, HG, DH2, D).transpose(0, 2, 1, 3),
        "bias": arr(L0_xattn_position_bias).reshape(NG, HG, T, T).transpose(0, 2, 1, 3),
        "mask": arr(mask_BxSxS2_bk0).transpose(1, 0, 2),
        "lnw": arr(L0_xattn_ln_weight),
        "wbase": chunks(arr(L0_ffn_W_base).T).reshape(P, -1),
        "war": chunks(np.concatenate([arr(L0_ffn_lora_A).reshape(E * RK, D), arr(L0_ffn_router_W)], axis=0).T)
        .reshape(P, -1),
        "wB": arr(L0_ffn_lora_B).transpose(0, 2, 1).reshape(E * RK, D),
        "b_base": rows(arr(L0_ffn_b_base)),
        "router_b": rows(arr(L0_ffn_router_b)),
        "prior": rows(arr(L0_ffn_domain_prior)),
        "active": arr(L0_ffn_active),
        "iota": rows(np.arange(E, dtype=np.float32)),
        "ident": np.eye(P, dtype=np.float32),
        "causal": np.where(tri, np.float32(0), np.float32(MASKED)),
        "rope": rope_tables(),
    }
    nc = bacc.Bacc("TRN2", target_bir_lowering=False, num_devices=1)
    ins, aps = {}, {}
    for name, v in arrays.items():
        ins[f"in_{name}"] = np.ascontiguousarray(v)
        aps[name] = nc.dram_tensor(f"in_{name}", v.shape, mybir.dt.from_np(v.dtype), kind="ExternalInput").ap()
    aps["out"] = nc.dram_tensor("out_0", (B, T, D), F32, kind="ExternalOutput").ap()
    build(nc, aps)
    r = run_bass_kernel_spmd(nc, [ins], core_ids=[0])
    return r.results[0]["out_0"]
```
